# Optimizing a Trainium2 kernel written in Bass

```python
import numpy as np
import jax
import jax.numpy as jnp

def _softmax(x, axis=-1):
    return jax.nn.softmax(x, axis=axis)

def _gelu(x):
    return jax.nn.gelu(x, approximate=True)

def _silu(x):
    return jax.nn.silu(x)

def _sigmoid(x):
    return jax.nn.sigmoid(x)

def _layernorm(x, axis=-1, eps=1e-05):
    m = jnp.mean(x, axis=axis, keepdims=True)
    v = jnp.var(x, axis=axis, keepdims=True)
    return (x - m) / jnp.sqrt(v + eps)

def _scatter_add(tgt, idx, src, axis=0):
    return tgt.at[idx].add(src)

def _segment_sum(src, seg, n):
    return jax.ops.segment_sum(src, seg, n)
kernel_name = 'mk_hybrid_d1_jaxref_r8_c18efc'

def setup_inputs(seed: int=0):
    np.random.seed(seed)
    _w = jnp.asarray

    def _L0_attn_a_setup():
        import jax, jax.numpy as jnp
        import numpy as np
        D_MODEL, N_STATE, E_INNER, K_CONV, DT_RANK = (128, 16, 256, 4, 64)
        EPS = 1e-06

        def _silu(x):
            return x * jax.nn.sigmoid(x)

        def _rmsnorm(x, w):
            var = jnp.mean(x * x, axis=-1, keepdims=True)
            return x * jax.lax.rsqrt(var + EPS) * w

        def _causal_dwconv(x, conv_w):
            xc = jnp.swapaxes(x, 1, 2)
            xc = jnp.pad(xc, ((0, 0), (0, 0), (K_CONV - 1, 0)))
            y = jax.lax.conv_general_dilated(xc, conv_w, window_strides=(1,), padding='VALID', dimension_numbers=('NCL', 'OIL', 'NCL'), feature_group_count=E_INNER)
            return jnp.swapaxes(y, 1, 2)

        def _selective_scan(u, delta, A, Bm, Cm, Dp):

            def step(h, inp):
                d_t, B_t, C_t, u_t = inp
                dA = jnp.exp(d_t[..., None] * A)
                h = dA * h + (d_t * u_t)[..., None] * B_t[:, None, :]
                y = jnp.einsum('ben,bn->be', h, C_t)
                return (h, y)
            h0 = jnp.zeros((u.shape[0], E_INNER, N_STATE), u.dtype)
            xs = (jnp.swapaxes(delta, 0, 1), jnp.swapaxes(Bm, 0, 1), jnp.swapaxes(Cm, 0, 1), jnp.swapaxes(u, 0, 1))
            h_last, ys = jax.lax.scan(step, h0, xs)
            return (jnp.swapaxes(ys, 0, 1) + u * Dp, h_last)

        def _reference_tuple_inner(hidden_states, norm_w, W_in, conv_w, W_x, W_dt, b_dt, A_log, D_param, W_out):
            residual = hidden_states
            x = _rmsnorm(hidden_states, norm_w)
            xz = jnp.einsum('bld,de->ble', x, W_in)
            x_in, z = jnp.split(xz, 2, axis=-1)
            x_act = _silu(_causal_dwconv(x_in, conv_w))
            x_db = jnp.einsum('ble,er->blr', x_act, W_x)
            dt_lr = x_db[..., :DT_RANK]
            Bm = x_db[..., DT_RANK:DT_RANK + N_STATE]
            Cm = x_db[..., DT_RANK + N_STATE:]
            delta = jax.nn.softplus(jnp.einsum('blr,re->ble', dt_lr, W_dt) + b_dt)
            A = -jnp.exp(A_log)
            y, h_last = _selective_scan(x_act, delta, A, Bm, Cm, D_param)
            y = y * _silu(z)
            out = jnp.einsum('ble,ed->bld', y, W_out)
            return (residual + out, h_last)
        key = jax.random.key(seed)
        ks = jax.random.split(key, 8)
        B, L = (4, 128)
        hidden_states = jax.random.normal(ks[0], (B, L, D_MODEL), jnp.float32)
        norm_w = jnp.ones((D_MODEL,), jnp.float32)
        W_in = jax.random.normal(ks[1], (D_MODEL, 2 * E_INNER), jnp.float32) * D_MODEL ** (-0.5)
        conv_w = jax.random.normal(ks[2], (E_INNER, 1, K_CONV), jnp.float32) * K_CONV ** (-0.5)
        W_x = jax.random.normal(ks[3], (E_INNER, DT_RANK + 2 * N_STATE), jnp.float32) * E_INNER ** (-0.5)
        W_dt = jax.random.normal(ks[4], (DT_RANK, E_INNER), jnp.float32) * DT_RANK ** (-0.5)
        dt = jnp.exp(jax.random.uniform(ks[5], (E_INNER,)) * (np.log(0.1) - np.log(0.001)) + np.log(0.001))
        b_dt = dt + jnp.log(-jnp.expm1(-dt))
        A_log = jnp.log(jnp.broadcast_to(jnp.arange(1, N_STATE + 1, dtype=jnp.float32), (E_INNER, N_STATE)))
        D_param = jnp.ones((E_INNER,), jnp.float32)
        W_out = jax.random.normal(ks[6], (E_INNER, D_MODEL), jnp.float32) * E_INNER ** (-0.5)
        return {'hidden_states': hidden_states, 'norm_w': norm_w, 'W_in': W_in, 'conv_w': conv_w, 'W_x': W_x, 'W_dt': W_dt, 'b_dt': b_dt, 'A_log': A_log, 'D_param': D_param, 'W_out': W_out}
    _L0_attn_a_in = _L0_attn_a_setup()

    def _L0_attn_b_setup():
        import jax, jax.numpy as jnp
        import numpy as np
        OUT_DIM = 128
        key = jax.random.key(seed)
        k1, k2, k3, k4 = jax.random.split(key, 4)
        B, N, D = (4, 256, 128)
        s = 1.0 / np.sqrt(D)
        return {'x': jax.random.normal(k1, (B, N, D), dtype=jnp.float32), 'W_query': jax.random.normal(k2, (D, OUT_DIM), dtype=jnp.float32) * s, 'W_key': jax.random.normal(k3, (D, OUT_DIM), dtype=jnp.float32) * s, 'W_value': jax.random.normal(k4, (D, OUT_DIM), dtype=jnp.float32) * s}
    _L0_attn_b_in = _L0_attn_b_setup()

    def _L0_ffn_setup():
        import jax, jax.numpy as jnp
        import numpy as np
        B, S, D_MODEL, D_FF = (4, 256, 128, 512)

        def _quantum_transform(hidden, theta, w_real, w_imag):
            imag = w_imag * jnp.sin(theta + hidden * 0.1)
            quantum_phase = jnp.cos(theta) * w_real + jnp.sin(theta) * w_imag
            return hidden + quantum_phase * imag * 0.1
        key = jax.random.key(seed)
        ks = jax.random.split(key, 8)
        return {'x': jax.random.normal(ks[0], (B, S, D_MODEL), dtype=jnp.float32), 'W1': jax.random.normal(ks[1], (D_MODEL, D_FF), dtype=jnp.float32) * (1.0 / np.sqrt(D_MODEL)), 'b1': jnp.zeros((D_FF,), dtype=jnp.float32), 'quantum_phases': jax.random.normal(ks[2], (D_FF,), dtype=jnp.float32) * (2.0 * np.pi), 'quantum_weights_real': jax.random.normal(ks[3], (D_FF,), dtype=jnp.float32) * 0.1, 'quantum_weights_imag': jax.random.normal(ks[4], (D_FF,), dtype=jnp.float32) * 0.1, 'W2': jax.random.normal(ks[5], (D_FF, D_MODEL), dtype=jnp.float32) * (1.0 / np.sqrt(D_FF)), 'b2': jnp.zeros((D_MODEL,), dtype=jnp.float32)}
    _L0_ffn_in = _L0_ffn_setup()
    _d = {'L0_attn_a_hidden_states': _L0_attn_a_in['hidden_states'], 'L0_attn_a_norm_w': _L0_attn_a_in['norm_w'], 'L0_attn_a_W_in': _L0_attn_a_in['W_in'], 'L0_attn_a_conv_w': _L0_attn_a_in['conv_w'], 'L0_attn_a_W_x': _L0_attn_a_in['W_x'], 'L0_attn_a_W_dt': _L0_attn_a_in['W_dt'], 'L0_attn_a_b_dt': _L0_attn_a_in['b_dt'], 'L0_attn_a_A_log': _L0_attn_a_in['A_log'], 'L0_attn_a_D_param': _L0_attn_a_in['D_param'], 'L0_attn_a_W_out': _L0_attn_a_in['W_out'], 'L0_attn_b_W_query': _L0_attn_b_in['W_query'], 'L0_attn_b_W_key': _L0_attn_b_in['W_key'], 'L0_attn_b_W_value': _L0_attn_b_in['W_value'], 'L0_ffn_W1': _L0_ffn_in['W1'], 'L0_ffn_b1': _L0_ffn_in['b1'], 'L0_ffn_quantum_phases': _L0_ffn_in['quantum_phases'], 'L0_ffn_quantum_weights_real': _L0_ffn_in['quantum_weights_real'], 'L0_ffn_quantum_weights_imag': _L0_ffn_in['quantum_weights_imag'], 'L0_ffn_W2': _L0_ffn_in['W2'], 'L0_ffn_b2': _L0_ffn_in['b2']}
    _x0 = _d['L0_attn_a_hidden_states']
    _d['L0_attn_a_hidden_states'] = jax.random.normal(jax.random.fold_in(jax.random.key(seed), 1), (2, 1024, 128), dtype=_x0.dtype)
    del _x0
    return _d

def reference(L0_attn_a_hidden_states, L0_attn_a_norm_w, L0_attn_a_W_in, L0_attn_a_conv_w, L0_attn_a_W_x, L0_attn_a_W_dt, L0_attn_a_b_dt, L0_attn_a_A_log, L0_attn_a_D_param, L0_attn_a_W_out, L0_attn_b_W_query, L0_attn_b_W_key, L0_attn_b_W_value, L0_ffn_W1, L0_ffn_b1, L0_ffn_quantum_phases, L0_ffn_quantum_weights_real, L0_ffn_quantum_weights_imag, L0_ffn_W2, L0_ffn_b2):

    def _L0_attn_a_ref(hidden_states, norm_w, W_in, conv_w, W_x, W_dt, b_dt, A_log, D_param, W_out):
        import jax, jax.numpy as jnp
        import numpy as np
        D_MODEL, N_STATE, E_INNER, K_CONV, DT_RANK = (128, 16, 256, 4, 64)
        EPS = 1e-06

        def _silu(x):
            return x * jax.nn.sigmoid(x)

        def _rmsnorm(x, w):
            var = jnp.mean(x * x, axis=-1, keepdims=True)
            return x * jax.lax.rsqrt(var + EPS) * w

        def _causal_dwconv(x, conv_w):
            xc = jnp.swapaxes(x, 1, 2)
            xc = jnp.pad(xc, ((0, 0), (0, 0), (K_CONV - 1, 0)))
            y = jax.lax.conv_general_dilated(xc, conv_w, window_strides=(1,), padding='VALID', dimension_numbers=('NCL', 'OIL', 'NCL'), feature_group_count=E_INNER)
            return jnp.swapaxes(y, 1, 2)

        def _selective_scan(u, delta, A, Bm, Cm, Dp):

            def step(h, inp):
                d_t, B_t, C_t, u_t = inp
                dA = jnp.exp(d_t[..., None] * A)
                h = dA * h + (d_t * u_t)[..., None] * B_t[:, None, :]
                y = jnp.einsum('ben,bn->be', h, C_t)
                return (h, y)
            h0 = jnp.zeros((u.shape[0], E_INNER, N_STATE), u.dtype)
            xs = (jnp.swapaxes(delta, 0, 1), jnp.swapaxes(Bm, 0, 1), jnp.swapaxes(Cm, 0, 1), jnp.swapaxes(u, 0, 1))
            h_last, ys = jax.lax.scan(step, h0, xs)
            return (jnp.swapaxes(ys, 0, 1) + u * Dp, h_last)

        def _reference_tuple_inner(hidden_states, norm_w, W_in, conv_w, W_x, W_dt, b_dt, A_log, D_param, W_out):
            residual = hidden_states
            x = _rmsnorm(hidden_states, norm_w)
            xz = jnp.einsum('bld,de->ble', x, W_in)
            x_in, z = jnp.split(xz, 2, axis=-1)
            x_act = _silu(_causal_dwconv(x_in, conv_w))
            x_db = jnp.einsum('ble,er->blr', x_act, W_x)
            dt_lr = x_db[..., :DT_RANK]
            Bm = x_db[..., DT_RANK:DT_RANK + N_STATE]
            Cm = x_db[..., DT_RANK + N_STATE:]
            delta = jax.nn.softplus(jnp.einsum('blr,re->ble', dt_lr, W_dt) + b_dt)
            A = -jnp.exp(A_log)
            y, h_last = _selective_scan(x_act, delta, A, Bm, Cm, D_param)
            y = y * _silu(z)
            out = jnp.einsum('ble,ed->bld', y, W_out)
            return (residual + out, h_last)
        return _reference_tuple_inner(hidden_states, norm_w, W_in, conv_w, W_x, W_dt, b_dt, A_log, D_param, W_out)[0]

    def _L0_attn_b_ref(x, W_query, W_key, W_value):
        import jax, jax.numpy as jnp
        import numpy as np
        OUT_DIM = 128
        q = jnp.einsum('bnd,de->bne', x, W_query)
        k = jnp.einsum('bnd,de->bne', x, W_key)
        v = jnp.einsum('bnd,de->bne', x, W_value)
        sqrt_d = jnp.sqrt(jnp.asarray(OUT_DIM, dtype=jnp.float32))
        scores = jnp.einsum('bie,bje->bij', q, k) / sqrt_d
        attn = jax.nn.softmax(scores, axis=1)
        return jnp.einsum('bij,bie->bje', attn, v)

    def _L0_ffn_ref(x, W1, b1, quantum_phases, quantum_weights_real, quantum_weights_imag, W2, b2):
        import jax, jax.numpy as jnp
        import numpy as np
        B, S, D_MODEL, D_FF = (4, 256, 128, 512)

        def _quantum_transform(hidden, theta, w_real, w_imag):
            imag = w_imag * jnp.sin(theta + hidden * 0.1)
            quantum_phase = jnp.cos(theta) * w_real + jnp.sin(theta) * w_imag
            return hidden + quantum_phase * imag * 0.1
        hidden = jnp.einsum('bsd,df->bsf', x, W1) + b1
        q = _quantum_transform(hidden, quantum_phases, quantum_weights_real, quantum_weights_imag)
        act = jax.nn.relu(q)
        return jnp.einsum('bsf,fd->bsd', act, W2) + b2
    x = L0_attn_a_hidden_states
    x = x + _L0_attn_a_ref(_layernorm(x, axis=-1), L0_attn_a_norm_w, L0_attn_a_W_in, L0_attn_a_conv_w, L0_attn_a_W_x, L0_attn_a_W_dt, L0_attn_a_b_dt, L0_attn_a_A_log, L0_attn_a_D_param, L0_attn_a_W_out)
    x = x + _L0_ffn_ref(_layernorm(x, axis=-1), L0_ffn_W1, L0_ffn_b1, L0_ffn_quantum_phases, L0_ffn_quantum_weights_real, L0_ffn_quantum_weights_imag, L0_ffn_W2, L0_ffn_b2)
    x = x + _L0_attn_b_ref(_layernorm(x, axis=-1), L0_attn_b_W_query, L0_attn_b_W_key, L0_attn_b_W_value)
    x = x + _L0_ffn_ref(_layernorm(x, axis=-1), L0_ffn_W1, L0_ffn_b1, L0_ffn_quantum_phases, L0_ffn_quantum_weights_real, L0_ffn_quantum_weights_imag, L0_ffn_W2, L0_ffn_b2)
    return x

_drawn_inputs = setup_inputs


def setup_inputs(seed=0):
    import zlib

    import numpy as np

    out = dict(_drawn_inputs(seed))
    spreads = {'L0_attn_a_norm_w': (1.0, 0.2),
     'L0_attn_a_D_param': (1.0, 0.6),
     'L0_ffn_b1': (0.0, 0.8),
     'L0_ffn_b2': (0.0, 0.8)}
    factors = {'L0_attn_a_W_dt': 12.13,
     'L0_attn_a_b_dt': 15.993,
     'L0_attn_a_A_log': 15.059,
     'L0_ffn_quantum_phases': 64.0,
     'L0_ffn_quantum_weights_real': 200.0,
     'L0_ffn_quantum_weights_imag': 64.0,
     'L0_attn_a_W_x': 3.913,
     'L0_attn_b_W_query': 8.0,
     'L0_attn_b_W_key': 8.0,
     'L0_attn_b_W_value': 8.0,
     'L0_ffn_W1': 4.045,
     'L0_ffn_W2': 3.175}
    for name, (base, spread) in spreads.items():
        noise = np.random.default_rng([zlib.crc32(name.encode()), seed]).standard_normal(out[name].shape)
        drawn = base * np.exp(spread * noise) if base else spread * noise
        out[name] = jnp.asarray(drawn.astype(out[name].dtype))
    for name, factor in factors.items():
        out[name] = (out[name] * factor).astype(out[name].dtype)
    return out
```

```python
from contextlib import ExitStack

import numpy as np

import concourse.bass as bass
from concourse import mybir

ALU = mybir.AluOpType
ACT = mybir.ActivationFunctionType
AX_X = mybir.AxisListType.X
F32 = mybir.dt.float32
BF16 = mybir.dt.bfloat16

P = 128
BATCH, SEQ, D = 2, 1024, 128
TILES = SEQ // P
E, NST, RANK, KCONV = 256, 16, 64, 4
EH = E // P
F = 512
FC = F // P
CH = 512
NCH = SEQ // CH
TPC = CH // P
B3 = 96
SLOTS = 4
STEPS = NST * EH
LN_EPS, RMS_EPS = 1e-5, 1e-6

ROUND = 1.5 * 2.0 ** 23
TWO_PI = 2.0 * np.pi
INV_2PI = float(np.float32(1.0 / TWO_PI))
C1 = 6.28125
C2 = float(np.round((TWO_PI - C1) * 2.0 ** 20) / 2.0 ** 20)
C3 = float(TWO_PI - C1 - C2)
PI_LO = float(np.nextafter(np.float32(np.pi), np.float32(0)))
ATANH = (2.0000000076817575, 0.6666632164139702, 0.4002459522991947, 0.27965157756134756, 0.28157778314218707)


def build(nc, hidden, norm_w, w_in, conv_w, w_x, w_dt, b_dt, a_log, d_param, w_out,
          w_q, w_k, w_v, w1, b1, phases, q_real, q_imag, w2, b2, out):
    with ExitStack() as ctx:
        def sb(name, shape, dt=F32):
            return ctx.enter_context(nc.sbuf_tensor(name, shape, dt))

        def sem(name):
            return ctx.enter_context(nc.semaphore(name))

        x_tok = sb("x_tok", [P, BATCH * TILES, D])
        xn = sb("xn", [P, TILES, D])
        x1 = sb("x1", [P, TILES, D])
        xnT = sb("xnT", [P, SEQ])
        win_sb = sb("win_sb", [P, 2 * E])
        wx_sb = sb("wx_sb", [P, EH, RANK + 2 * NST])
        wdt_sb = sb("wdt_sb", [RANK, E])
        wout_sb = sb("wout_sb", [P, EH, D])
        w1_sb = sb("w1_sb", [P, F])
        w2_sb = sb("w2_sb", [P, FC, D])
        wq_sb = sb("wq_sb", [P, D])
        wk_sb = sb("wk_sb", [P, D])
        wv_sb = sb("wv_sb", [P, D])
        normw_sb = sb("normw_sb", [P, 1])
        convw_sb = sb("convw_sb", [P, EH, KCONV])
        bdt_sb = sb("bdt_sb", [P, EH])
        dpar_sb = sb("dpar_sb", [P, EH])
        a_sb = sb("a_sb", [P, EH, NST])
        b1_sb = sb("b1_sb", [P, FC])
        theta = sb("theta", [P, FC])
        wr_sb = sb("wr_sb", [P, FC])
        wi_sb = sb("wi_sb", [P, FC])
        b2_sb = sb("b2_sb", [P, D])
        rho = sb("rho", [P, FC])
        trig = sb("trig", [P, 8, FC])
        coef = sb("coef", [P, FC])
        ident = sb("ident", [P, P])
        bsel = sb("bsel", [B3, NST, P], BF16)
        wb3_sb = sb("wb3_sb", [P, EH, B3])
        b3 = sb("b3", [B3, SEQ], BF16)
        b3_rest = sb("b3_rest", [B3, SEQ])
        b3_mid = sb("b3_mid", [B3, SEQ], BF16)
        two = sb("two", [P, 1])

        stats = sb("stats", [P, TILES, 6])
        mv = sb("mv", [P, TILES, 2])
        var_eps = sb("var_eps", [P, TILES])
        lnv = sb("lnv", [P, TILES])
        rstd0 = sb("rstd0", [P, TILES])
        newton = sb("newton", [P, TILES])
        rstd = sb("rstd", [P, TILES])
        rstd2 = sb("rstd2", [P, TILES])

        xin = sb("xin", [P, EH, KCONV - 1 + SEQ])
        conv = sb("conv", [P, EH, SEQ])
        u = sb("u", [P, EH, SEQ])
        zs = sb("zs", [P, EH, SEQ])
        xdb = sb("xdb", [RANK + 2 * NST, SEQ])
        delta = sb("delta", [P, EH, SEQ])
        du = sb("du", [P, EH, SEQ])
        ebuf = sb("ebuf", [P, EH, SEQ])
        sbuf_ = sb("sbuf_", [P, EH, SEQ])
        s2buf = sb("s2buf", [P, EH, SEQ])
        c_all = sb("c_all", [P, NST, CH])
        dbu = sb("dbu", [P, SLOTS, CH])
        hs = sb("hs", [P, SLOTS, CH])
        prod = sb("prod", [P, SLOTS, CH])
        state = sb("state", [P, STEPS])
        y2 = sb("y2", [P, EH, CH])

        hid = ebuf[:, :, :].rearrange("p h (s t) -> p (h s) t", t=CH)
        tbuf = sbuf_[:, :, :].rearrange("p h (s t) -> p (h s) t", t=CH)
        sarg = s2buf[:, :, :].rearrange("p h (s t) -> p (h s) t", t=CH)
        jbuf = sb("jbuf", [P, SLOTS, CH])
        sn = sb("sn", [P, SLOTS, CH])
        act_sb = sb("act_sb", [P, SLOTS, CH])

        qT = du[:, 0, :]
        kT = du[:, 1, :]
        vt = conv[:, 0, :].rearrange("p (i d) -> p i d", d=D)
        pm = jbuf[:, :, :].rearrange("p (a s) t -> p a (s t)", a=2)
        pT = sn[:, :, :].rearrange("p (a s) (i d) -> p a (s i) d", a=2, d=P)
        mx = sb("mx", [P, 2])
        negm = sb("negm", [P, 2])
        rsum = sb("rsum", [P, 2])
        rinv = sb("rinv", [P, 2])

        c_dram = nc.dram_tensor("c_scratch", [BATCH, NST, SEQ], F32, kind="Internal").ap()
        ps = ctx.enter_context(nc.psum_tensor("ps", [P, 8, CH], F32))

        x_loaded = [sem(f"x_loaded{b}") for b in range(BATCH)]
        mamba_w_loaded = sem("mamba_w_loaded")
        small_w_loaded = sem("small_w_loaded")
        late_w_loaded = sem("late_w_loaded")
        consts_made = sem("consts_made")
        pool_chain = sem("pool_chain")
        act_chain = sem("act_chain")
        dve_chain = sem("dve_chain")
        win_scaled = sem("win_scaled")
        trig_args = sem("trig_args")
        trig_done = sem("trig_done")
        a_exp = sem("a_exp")
        a_ready = sem("a_ready")
        var_ready = sem("var_ready")
        rstd_guess = sem("rstd_guess")
        xn_ready = sem("xn_ready")
        xT_in_psum = sem("xT_in_psum")
        xnT_ready = sem("xnT_ready")
        resid_added = sem("resid_added")
        inproj_done = sem("inproj_done")
        xin_ready = sem("xin_ready")
        z_ready = sem("z_ready")
        conv_ready = sem("conv_ready")
        u_ready = sem("u_ready")
        xdb_in_psum = sem("xdb_in_psum")
        xdb_ready = sem("xdb_ready")
        wb3_ready = sem("wb3_ready")
        b3_in_psum = sem("b3_in_psum")
        b3_high = sem("b3_high")
        b3_rest_ready = sem("b3_rest_ready")
        b3_mid_ready = sem("b3_mid_ready")
        b3_ready = sem("b3_ready")
        dt_in_psum = sem("dt_in_psum")
        e_ready = sem("e_ready")
        relu_part = sem("relu_part")
        s_ready = sem("s_ready")
        s2_ready = sem("s2_ready")
        log1p_ready = sem("log1p_ready")
        du_ready = sem("du_ready")
        c_stored = sem("c_stored")
        c_loaded = sem("c_loaded")
        dA_ready = sem("dA_ready")
        B_ready = sem("B_ready")
        dbu_ready = sem("dbu_ready")
        h_ready = sem("h_ready")
        prod_ready = sem("prod_ready")
        y_added = sem("y_added")
        y_read = sem("y_read")
        y2_ready = sem("y2_ready")
        mamba_out = sem("mamba_out")
        hid_in_psum = sem("hid_in_psum")
        hid_ready = sem("hid_ready")
        turns_ready = sem("turns_ready")
        arg_ready = sem("arg_ready")
        sin_ready = sem("sin_ready")
        act_ready = sem("act_ready")
        act_used = sem("act_used")
        qkv_in_psum = sem("qkv_in_psum")
        qv_ready = sem("qv_ready")
        k_ready = sem("k_ready")
        scores_ready = sem("scores_ready")
        mx_ready = sem("mx_ready")
        rinv_ready = sem("rinv_ready")
        negm_ready = sem("negm_ready")
        probs_ready = sem("probs_ready")
        pT_in_psum = sem("pT_in_psum")
        pT_act = sem("pT_act")
        pT_dve = sem("pT_dve")
        attn_out = sem("attn_out")
        attn_added = sem("attn_added")
        x_final = sem("x_final")
        stored = sem("stored")

        class Chain:
            def __init__(self, eng, s):
                self.eng, self.s, self.n = eng, s, 0

            def add(self, ins):
                ins.then_inc(self.s, 1)
                self.n += 1

            def wait(self):
                self.eng.wait_ge(self.s, self.n)

            def link(self, ins):
                self.add(ins)
                self.wait()

        x_dram = hidden.rearrange("b (t p) d -> b p t d", p=P)
        out_dram = out.rearrange("b (t p) d -> b p t d", p=P)

        def x_of(b):
            return x_tok[:, b * TILES:(b + 1) * TILES, :]

        win_v = win_sb[:, :].rearrange("k (s p c) -> k s c p", s=2, c=EH)
        wdt_v = wdt_sb[:, :].rearrange("k (p c) -> k c p", c=EH)
        w1_v = w1_sb[:, :].rearrange("k (p c) -> k c p", c=FC)
        N_SMALL = 5
        N_MAMBA = 5
        N_LATE = 9

        block = ctx.enter_context(nc.Block())

        @block.sync
        def _(sp):
            sp.dma_start(x_of(0), x_dram[0]).then_inc(x_loaded[0], 16)
            sp.dma_start(win_sb[:, :], w_in).then_inc(mamba_w_loaded, 16)
            sp.dma_start(normw_sb[:, :], norm_w.rearrange("(p o) -> p o", o=1)).then_inc(mamba_w_loaded, 16)
            sp.dma_start(wx_sb[:, :, :], w_x.rearrange("(p c) r -> p c r", c=EH)).then_inc(mamba_w_loaded, 16)
            sp.dma_start(wdt_sb[:, :], w_dt).then_inc(mamba_w_loaded, 16)
            sp.dma_start(wout_sb[:, :, :], w_out.rearrange("(p c) d -> p c d", c=EH)).then_inc(mamba_w_loaded, 16)
            sp.dma_start(convw_sb[:, :, :], conv_w.rearrange("(p c) o k -> p c (o k)", c=EH)).then_inc(small_w_loaded, 16)
            sp.dma_start(a_sb[:, :, :], a_log.rearrange("(p c) n -> p c n", c=EH)).then_inc(small_w_loaded, 16)
            sp.dma_start(bdt_sb[:, :], b_dt.rearrange("(p c) -> p c", c=EH)).then_inc(small_w_loaded, 16)
            sp.dma_start(dpar_sb[:, :], d_param.rearrange("(p c) -> p c", c=EH)).then_inc(small_w_loaded, 16)
            sp.dma_start(theta[:, :], phases.rearrange("(p c) -> p c", c=FC)).then_inc(small_w_loaded, 16)
            sp.dma_start(x_of(1), x_dram[1]).then_inc(x_loaded[1], 16)
            for dst, src in ((b1_sb, b1), (wr_sb, q_real), (wi_sb, q_imag)):
                sp.dma_start(dst[:, :], src.rearrange("(p c) -> p c", c=FC)).then_inc(late_w_loaded, 16)
            sp.dma_start(b2_sb[:, :], b2.partition_broadcast(P)).then_inc(late_w_loaded, 16)
            sp.dma_start(w1_sb[:, :], w1).then_inc(late_w_loaded, 16)
            sp.dma_start(w2_sb[:, :, :], w2.rearrange("(p c) d -> p c d", c=FC)).then_inc(late_w_loaded, 16)
            for dst, src in ((wq_sb, w_q), (wk_sb, w_k), (wv_sb, w_v)):
                sp.dma_start(dst[:, :], src).then_inc(late_w_loaded, 16)
            for b in range(BATCH):
                sp.wait_ge(xdb_ready, 2 * b + 2)
                sp.dma_start(c_dram[b], xdb[RANK + NST:RANK + 2 * NST, :]).then_inc(c_stored, 16)
                sp.wait_ge(c_stored, 16 * (b + 1))
                for c in range(NCH):
                    q = b * NCH + c
                    for g in range(NST // 2):
                        if q:
                            sp.wait_ge(prod_ready, STEPS * (q - 1) + 4 * (g + 1))
                        src = c_dram[b, 2 * g:2 * g + 2, c * CH:(c + 1) * CH].partition_broadcast(P)
                        sp.dma_start(c_all[:, 2 * g:2 * g + 2, :], src).then_inc(c_loaded, 16)
                        sp.wait_ge(c_loaded, 16 * (q * NST // 2 + g + 1))
            for b in range(BATCH):
                sp.wait_ge(x_final, b + 1)
                sp.dma_start(out_dram[b], x_of(b)).then_inc(stored, 16)
            sp.wait_ge(stored, 16 * BATCH)

        @block.gpsimd
        def _(pool):
            chain = Chain(pool, pool_chain)
            g = nc.gpsimd
            g.memset(two[:, :], 2.0).then_inc(consts_made, 1)
            chain.add(g.memset(ident[:, :], 0.0))
            chain.link(g.memset(bsel[:, :, :], 0.0))
            g.affine_select(out=ident[:, :], in_=ident[:, :], compare_op=ALU.not_equal, fill=1.0, base=0,
                            pattern=[[-1, P]], channel_multiplier=1).then_inc(consts_made, 1)
            for part in range(3):
                ins = g.affine_select(out=bsel[:, :, :], in_=bsel[:, :, :], compare_op=ALU.not_equal, fill=1.0,
                                      base=-32 * part, pattern=[[-1, NST], [0, P]], channel_multiplier=1)
                if part < 2:
                    chain.link(ins)
            ins.then_inc(consts_made, 1)
            chain.link(g.memset(wb3_sb[:, :, :], 0.0))
            pool.wait_ge(mamba_w_loaded, 16 * N_MAMBA)
            for part in range(3):
                ins = g.tensor_copy(wb3_sb[:, :, 32 * part:32 * part + NST], wx_sb[:, :, RANK:RANK + NST])
            ins.then_inc(wb3_ready, 1)

            def scan_pair(q, c, i):
                pool.wait_ge(c_loaded, 16 * (i + (q * NST // 2 + 1)))
                for j in range(2 * EH):
                    k = i * 4 + (q * STEPS + j)
                    n = i * 2 + j // EH
                    pool.wait_ge(h_ready, k + 1)
                    if not (q == 0 and isinstance(i, int) and i == 0):
                        pool.wait_ge(y_added, k - (SLOTS - 1))
                    pool.nop(nofuse=True)
                    if c == 0:
                        g.tensor_copy(state[:, bass.ds(i * 4 + j, 1)], hs[:, j, CH - 1:CH])
                    g.tensor_tensor(prod[:, j, :], hs[:, j, :], c_all[:, bass.ds(n, 1), :].rearrange("p o t -> p (o t)"), ALU.mult)\
                        .then_inc(prod_ready, 1)

            def ffn(b, l, idx):
                pool.wait_ge(xn_ready, 2 * l + 2)
                g.tensor_tensor(x_of(b), x_of(b), b2_sb[:, :].unsqueeze(1).to_broadcast([P, TILES, D]), ALU.add)\
                    .then_inc(resid_added, 1)
                for v in range(8):
                    U = idx * 8 + v
                    sl = U % SLOTS
                    pool.wait_ge(turns_ready, U + 1)
                    chain.link(g.tensor_tensor(jbuf[:, sl, :], jbuf[:, sl, :], sarg[:, sl, :], ALU.add))
                    g.tensor_scalar(jbuf[:, sl, :], jbuf[:, sl, :], PI_LO, -PI_LO, ALU.min, ALU.max).then_inc(arg_ready, 1)

            for b in range(BATCH):
                l = 4 * b
                pool.wait_ge(xn_ready, 2 * l + 2)
                g.tensor_tensor(x_of(b), x_of(b), x1[:, :, :], ALU.add).then_inc(resid_added, 1)
                for h in range(EH):
                    pool.wait_ge(e_ready, 2 * EH * b + 2 * h + 2)
                    g.tensor_tensor(sbuf_[:, h, :], ebuf[:, h, :], sbuf_[:, h, :], ALU.mult).then_inc(s_ready, 1)
                for h in range(EH):
                    pool.wait_ge(log1p_ready, EH * b + h + 1)
                    chain.link(g.tensor_tensor(delta[:, h, :], delta[:, h, :], s2buf[:, h, :], ALU.add))
                    g.tensor_tensor(du[:, h, :], delta[:, h, :], u[:, h, :], ALU.mult).then_inc(du_ready, 1)
                for c in range(NCH):
                    q = b * NCH + c
                    scan_pair(q, c, 0)
                    with pool.Fori(1, NST // 2) as i:
                        scan_pair(q, c, i)
                ffn(b, l + 1, 2 * b)
                ffn(b, l + 3, 2 * b + 1)

        @block.scalar
        def _(act):
            chain = Chain(act, act_chain)
            s = nc.scalar

            def layer_norm_root(m):
                act.wait_ge(var_ready, m + 1)
                chain.link(s.activation(lnv[:, :], var_eps[:, :], ACT.Ln))
                s.activation(rstd0[:, :], lnv[:, :], ACT.Exp, scale=-0.5).then_inc(rstd_guess, 1)

            def xT_copies(l):
                for t in range(2):
                    act.wait_ge(xT_in_psum, 2 * l + t + 1)
                    s.copy(xnT[:, t * CH:(t + 1) * CH], ps[:, t, :]).then_inc(xnT_ready, 1)

            def scan_pair(q, c, i):
                for j in range(2 * EH):
                    k = i * 4 + (q * STEPS + j)
                    n = i * 2 + j // EH
                    h = j % EH
                    if not (q == 0 and isinstance(i, int) and i == 0 and j < 2):
                        act.wait_ge(h_ready, k - 1)
                    s.activation(ps[:, h, :], delta[:, h, c * CH:(c + 1) * CH], ACT.Exp,
                                 scale=a_sb[:, h, bass.ds(n, 1)]).then_inc(dA_ready, 1)

            def ffn(b, idx):
                s.preload_act_table_set("silu_and_others")

                def evict(v):
                    U = idx * 8 + v
                    act.wait_ge(hid_in_psum, U + 1)
                    if U >= SLOTS:
                        act.wait_ge(act_ready, U - SLOTS + 1)
                    s.activation(hid[:, U % SLOTS, :], ps[:, 2 + v % 2, :], ACT.Identity,
                                 bias=b1_sb[:, v % FC:v % FC + 1]).then_inc(hid_ready, 1)

                def sine(v):
                    U = idx * 8 + v
                    act.wait_ge(arg_ready, U + 1)
                    if U >= SLOTS:
                        act.wait_ge(act_ready, U - SLOTS + 1)
                    s.activation(sn[:, U % SLOTS, :], jbuf[:, U % SLOTS, :], ACT.Sin).then_inc(sin_ready, 1)

                for v in range(8 + 2):
                    if v < 8:
                        evict(v)
                    if v >= 2:
                        sine(v - 2)
                s.preload_act_table_set("natural_log_exp_and_others")

            def attention(b):
                for t in range(2):
                    act.wait_ge(qkv_in_psum, 6 * b + t + 1)
                    s.copy(qT[:, t * CH:(t + 1) * CH], ps[:, 2 + t, :]).then_inc(qv_ready, 1)
                for t in range(2):
                    act.wait_ge(qkv_in_psum, 6 * b + t + 5)
                    s.copy(vt[:, 4 * t:4 * t + 4, :].rearrange("p t d -> p (t d)"), ps[:, 6 + t, :]).then_inc(qv_ready, 1)

                def tile(i, par, first):
                    J = i * 2 + (b * TILES + par)
                    act.wait_ge(negm_ready, J + 1)
                    if not first:
                        act.wait_ge(pT_in_psum, 2 * J - 2)
                        act.wait_ge(attn_added, J - 1)
                    s.activation(pm[:, par, :], ps[:, 2 * par:2 * par + 2, :].rearrange("p a t -> p (a t)"), ACT.Exp,
                                 bias=negm[:, par:par + 1], scale=float(1.0 / np.sqrt(D)),
                                 accum_out=rsum[:, par:par + 1]).then_inc(probs_ready, 1)
                    act.wait_ge(pT_in_psum, 2 * J + 1)
                    if not first:
                        act.wait_ge(attn_out, J - 1)
                    s.copy(pT[:, par, 0:4, :].rearrange("p t d -> p (t d)"), ps[:, 4, :]).then_inc(pT_act, 1)

                for par in range(2):
                    tile(0, par, b == 0)
                with act.Fori(1, TILES // 2) as i:
                    for par in range(2):
                        tile(i, par, False)

            s.preload_act_table_set("silu_and_others")
            act.wait_ge(trig_args, 1)
            s.activation(trig[:, 4:6, :], trig[:, 0:2, :], ACT.Sin).then_inc(trig_done, 1)
            s.preload_act_table_set("natural_log_exp_and_others")
            act.wait_ge(small_w_loaded, 16 * N_SMALL)
            s.activation(a_sb[:, :, :], a_sb[:, :, :], ACT.Exp).then_inc(a_exp, 1)
            m = 0
            for b in range(BATCH):
                l = 4 * b
                layer_norm_root(m)
                layer_norm_root(m + 1)
                m += 2
                xT_copies(l)
                s.preload_act_table_set("silu_and_others")
                for h in range(EH):
                    for t in range(2):
                        act.wait_ge(inproj_done, 8 * b + 2 * h + t + 1)
                        o = KCONV - 1 + t * CH
                        s.copy(xin[:, h, o:o + CH], ps[:, 2 + 2 * h + t, :]).then_inc(xin_ready, 1)
                for h in range(EH):
                    for t in range(2):
                        act.wait_ge(inproj_done, 8 * b + 4 + 2 * h + t + 1)
                        s.activation(zs[:, h, t * CH:(t + 1) * CH], ps[:, (6 + 2 * h + t) % 8, :], ACT.Silu).then_inc(z_ready, 1)
                for h in range(EH):
                    act.wait_ge(conv_ready, EH * b + h + 1)
                    s.activation(u[:, h, :], conv[:, h, :], ACT.Silu).then_inc(u_ready, 1)
                s.preload_act_table_set("natural_log_exp_and_others")
                for t in range(2):
                    act.wait_ge(xdb_in_psum, 2 * b + t + 1)
                    s.copy(xdb[:, t * CH:(t + 1) * CH], ps[0:RANK + 2 * NST, 2 + t, :]).then_inc(xdb_ready, 1)
                act.wait_ge(b3_in_psum, b + 1)
                s.copy(b3[:, :], ps[0:B3, 0:2, :].rearrange("p a t -> p (a t)")).then_inc(b3_high, 1)
                act.wait_ge(b3_rest_ready, b + 1)
                s.copy(b3[32:64, :], b3_rest[32:64, :]).then_inc(b3_mid_ready, 1)
                s.copy(b3_mid[64:96, :], b3_rest[64:96, :]).then_inc(b3_mid_ready, 1)
                for h in range(EH):
                    act.wait_ge(dt_in_psum, 2 * EH * b + 2 * h + 2)
                    v = ps[:, 4 + 2 * h:6 + 2 * h, :].rearrange("p a t -> p (a t)")
                    chain.link(s.activation(ebuf[:, h, :], v, ACT.Abs, bias=bdt_sb[:, h:h + 1]))
                    s.activation(ebuf[:, h, :], ebuf[:, h, :], ACT.Exp, scale=-1.0).then_inc(e_ready, 1)
                    act.wait_ge(e_ready, 2 * EH * b + 2 * h + 1)
                    chain.link(s.activation(sbuf_[:, h, :], ebuf[:, h, :], ACT.Ln, bias=two[:, :]))
                    s.activation(sbuf_[:, h, :], sbuf_[:, h, :], ACT.Exp, scale=-1.0).then_inc(e_ready, 1)
                for h in range(EH):
                    act.wait_ge(s_ready, EH * b + h + 1)
                    s.activation(s2buf[:, h, :], sbuf_[:, h, :], ACT.Square).then_inc(s2_ready, 1)
                act.wait_ge(a_ready, 1)
                act.wait_ge(du_ready, EH * b + EH)
                for c in range(NCH):
                    q = b * NCH + c
                    scan_pair(q, c, 0)
                    with act.Fori(1, NST // 2) as i:
                        scan_pair(q, c, i)
                layer_norm_root(m)
                xT_copies(l + 1)
                ffn(b, 2 * b)
                layer_norm_root(m + 1)
                xT_copies(l + 2)
                attention(b)
                layer_norm_root(m + 2)
                xT_copies(l + 3)
                ffn(b, 2 * b + 1)
                m += 3

        @block.vector
        def _(dve):
            chain = Chain(dve, dve_chain)
            v_ = nc.vector

            def newton_step(m, dst):
                dve.wait_ge(rstd_guess, m + 1)
                chain.link(v_.tensor_tensor(newton[:, :], rstd0[:, :], rstd0[:, :], ALU.mult))
                chain.link(v_.tensor_tensor(newton[:, :], newton[:, :], var_eps[:, :], ALU.mult))
                chain.link(v_.tensor_scalar(newton[:, :], newton[:, :], -0.5, 1.5, ALU.mult, ALU.add))
                chain.link(v_.tensor_tensor(dst[:, :], rstd0[:, :], newton[:, :], ALU.mult))

            def layer_norm(b, m, rms):
                xb = x_of(b)
                for t in range(TILES):
                    chain.add(v_.bn_stats(stats[:, t, :], xb[:, t, :]))
                chain.wait()
                for t in range(TILES):
                    chain.add(v_.bn_aggr(mv[:, t, :], stats[:, t, :]))
                chain.wait()
                v_.tensor_scalar(var_eps[:, :], mv[:, :, 1], LN_EPS, None, ALU.add).then_inc(var_ready, 1)
                newton_step(m, rstd)
                scale = rstd
                if rms:
                    chain.link(v_.tensor_tensor(newton[:, :], rstd[:, :], rstd[:, :], ALU.mult))
                    chain.link(v_.tensor_tensor(newton[:, :], newton[:, :], mv[:, :, 1], ALU.mult))
                    v_.tensor_scalar(var_eps[:, :], newton[:, :], RMS_EPS, None, ALU.add).then_inc(var_ready, 1)
                    for t in range(TILES):
                        v_.tensor_scalar(x1[:, t, :], xb[:, t, :], mv[:, t, 0:1], rstd[:, t:t + 1], ALU.subtract, ALU.mult)
                    newton_step(m + 1, rstd2)
                    chain.link(v_.tensor_tensor(rstd2[:, :], rstd2[:, :], rstd[:, :], ALU.mult))
                    scale = rstd2
                for t in range(TILES):
                    ins = v_.tensor_scalar(xn[:, t, :], xb[:, t, :], mv[:, t, 0:1], scale[:, t:t + 1], ALU.subtract, ALU.mult)
                    if t % 4 == 3:
                        ins.then_inc(xn_ready, 1)

            def dbu_step(c, i, j, q):
                n_ready = i * 2 + (q * NST + j // EH + 1)
                dve.wait_ge(B_ready, n_ready)
                v_.tensor_tensor(dbu[:, j, :], ps[:, 2 + j // EH, :], du[:, j % EH, c * CH:(c + 1) * CH], ALU.mult)\
                    .then_inc(dbu_ready, 1)

            def scan_step(c, i, j, q):
                k = i * 4 + (q * STEPS + j)
                dve.wait_ge(dbu_ready, k + 1)
                dve.wait_ge(dA_ready, k + 1)
                if not (q == 0 and isinstance(i, int) and i == 0):
                    dve.wait_ge(prod_ready, k - (SLOTS - 1))
                initial = 0.0 if c == 0 else state[:, bass.ds(i * 4 + j, 1)]
                v_.tensor_tensor_scan(hs[:, j, :], ps[:, j % EH, :], dbu[:, j, :], initial, ALU.mult, ALU.add)\
                    .then_inc(h_ready, 1)

            def scan_pair(q, c, i, last):
                for j in range(2 * EH):
                    if j < 2 * EH - 1:
                        dbu_step(c, i, j + 1, q)
                    elif not last:
                        dbu_step(c, i + 1, 0, q)
                    scan_step(c, i, j, q)

            def ffn(b, idx, l):
                def args(v):
                    U = idx * 8 + v
                    sl, f = U % SLOTS, v % FC
                    th = theta[:, f:f + 1]
                    dve.wait_ge(hid_ready, U + 1)
                    if U >= SLOTS:
                        dve.wait_ge(sin_ready, U - SLOTS + 1)
                    chain.link(v_.tensor_scalar(tbuf[:, sl, :], hid[:, sl, :], 0.1, th, ALU.mult, ALU.add))
                    chain.link(v_.tensor_scalar(sarg[:, sl, :], tbuf[:, sl, :], th, rho[:, f:f + 1], ALU.subtract, ALU.add))
                    chain.link(v_.tensor_scalar(jbuf[:, sl, :], sarg[:, sl, :], INV_2PI, ROUND, ALU.mult, ALU.add))
                    v_.tensor_scalar(jbuf[:, sl, :], jbuf[:, sl, :], ROUND, -TWO_PI, ALU.subtract, ALU.mult).then_inc(turns_ready, 1)

                def finish(v):
                    U = idx * 8 + v
                    sl, f = U % SLOTS, v % FC
                    dve.wait_ge(sin_ready, U + 1)
                    if U >= SLOTS:
                        dve.wait_ge(act_used, U - SLOTS + 1)
                    chain.link(v_.scalar_tensor_tensor(act_sb[:, sl, :], sn[:, sl, :], coef[:, f:f + 1], hid[:, sl, :], ALU.mult, ALU.add))
                    v_.tensor_scalar(act_sb[:, sl, :], act_sb[:, sl, :], 0.0, None, ALU.max).then_inc(act_ready, 1)

                def add_out(t):
                    dve.wait_ge(act_used, idx * 8 + 4 * t + 4)
                    xs = x_of(b)[:, 4 * t:4 * t + 4, :].rearrange("p t d -> p (t d)")
                    chain.add(v_.tensor_tensor(xs, ps[:, 4 + t, :], xs, ALU.add))

                dve.wait_ge(resid_added, (3 * b + (2 if idx % 2 == 0 else 3)))
                for v in range(8 + 2):
                    if v < 8:
                        args(v)
                    if v >= 2:
                        finish(v - 2)
                    if v == 7:
                        add_out(0)
                add_out(1)
                chain.wait()

            def attention(b):
                for t in range(2):
                    dve.wait_ge(qkv_in_psum, 6 * b + t + 3)
                    v_.tensor_copy(kT[:, t * CH:(t + 1) * CH], ps[:, 4 + t, :]).then_inc(k_ready, 1)

                def row_max(i, par):
                    J = i * 2 + (b * TILES + par)
                    dve.wait_ge(scores_ready, J + 1)
                    v_.tensor_reduce(mx[:, par:par + 1], ps[:, 2 * par:2 * par + 2, :].rearrange("p a t -> p (a t)"), AX_X, ALU.max)\
                        .then_inc(mx_ready, 1)
                    dve.wait_ge(mx_ready, J + 1)
                    v_.tensor_scalar(negm[:, par:par + 1], mx[:, par:par + 1], float(-1.0 / np.sqrt(D)), None, ALU.mult)\
                        .then_inc(negm_ready, 1)

                def rest(i, par, first):
                    J = i * 2 + (b * TILES + par)
                    dve.wait_ge(pT_in_psum, 2 * J + 2)
                    if not first:
                        dve.wait_ge(attn_out, J - 1)
                    v_.tensor_copy(pT[:, par, 4:8, :].rearrange("p t d -> p (t d)"), ps[:, 5, :]).then_inc(pT_dve, 1)
                    v_.reciprocal(rinv[:, par:par + 1], rsum[:, par:par + 1]).then_inc(rinv_ready, 1)
                    dve.wait_ge(rinv_ready, J + 1)
                    dve.wait_ge(attn_out, J + 1)
                    xs = x_tok[:, bass.ds(J, 1), :].rearrange("p o d -> p (o d)")
                    v_.scalar_tensor_tensor(xs, ps[:, 6 + par, 0:D], rinv[:, par:par + 1], xs, ALU.mult, ALU.add)\
                        .then_inc(attn_added, 1)

                row_max(0, 0)
                row_max(0, 1)
                rest(0, 0, b == 0)
                with dve.Fori(1, TILES // 2) as i:
                    row_max(i, 0)
                    rest(i - 1, 1, False) if b else rest(i - 1, 1, True)
                    row_max(i, 1)
                    rest(i, 0, False)
                rest(TILES // 2 - 1, 1, False)
                dve.wait_ge(attn_added, TILES * (b + 1))

            v_.memset(xin[:, :, 0:KCONV - 1], 0.0)
            dve.wait_ge(small_w_loaded, 16 * N_SMALL)
            kk, r = trig[:, 2, :], trig[:, 3, :]
            chain.link(v_.tensor_scalar(kk, theta[:, :], INV_2PI, ROUND, ALU.mult, ALU.add))
            chain.link(v_.tensor_scalar(kk, kk, ROUND, None, ALU.subtract))
            chain.link(v_.scalar_tensor_tensor(r, kk, -C1, theta[:, :], ALU.mult, ALU.add))
            chain.link(v_.scalar_tensor_tensor(r, kk, -C2, r, ALU.mult, ALU.add))
            chain.link(v_.scalar_tensor_tensor(rho[:, :], kk, -C3, r, ALU.mult, ALU.add))
            chain.link(v_.tensor_scalar(kk, rho[:, :], np.pi / 2, None, ALU.add))
            chain.link(v_.tensor_scalar(r, kk, np.pi, -TWO_PI, ALU.is_gt, ALU.mult))
            chain.link(v_.tensor_tensor(kk, kk, r, ALU.add))
            chain.add(v_.tensor_scalar(trig[:, 0, :], rho[:, :], PI_LO, -PI_LO, ALU.min, ALU.max))
            v_.tensor_scalar(trig[:, 1, :], kk, PI_LO, -PI_LO, ALU.min, ALU.max).then_inc(trig_args, 1)
            dve.wait_ge(a_exp, 1)
            v_.tensor_scalar(a_sb[:, :, :], a_sb[:, :, :], -1.0, None, ALU.mult).then_inc(a_ready, 1)
            dve.wait_ge(mamba_w_loaded, 16 * N_MAMBA)
            v_.tensor_scalar(win_sb[:, :], win_sb[:, :], normw_sb[:, :], None, ALU.mult).then_inc(win_scaled, 1)
            dve.wait_ge(late_w_loaded, 16 * N_LATE)
            dve.wait_ge(trig_done, 1)
            chain.link(v_.tensor_tensor(trig[:, 6, :], trig[:, 5, :], wr_sb[:, :], ALU.mult))
            chain.link(v_.tensor_tensor(trig[:, 7, :], trig[:, 4, :], wi_sb[:, :], ALU.mult))
            chain.link(v_.tensor_tensor(trig[:, 6, :], trig[:, 6, :], trig[:, 7, :], ALU.add))
            chain.link(v_.tensor_tensor(trig[:, 6, :], trig[:, 6, :], wi_sb[:, :], ALU.mult))
            chain.link(v_.tensor_scalar(coef[:, :], trig[:, 6, :], 0.1, None, ALU.mult))

            m = 0
            for b in range(BATCH):
                l = 4 * b
                dve.wait_ge(x_loaded[b], 16)
                layer_norm(b, m, True)
                m += 2
                for tap in range(KCONV - 1, -1, -1):
                    for h in range(EH):
                        if tap == KCONV - 1:
                            dve.wait_ge(xin_ready, 4 * b + 2 * h + 2)
                        src = xin[:, h, tap:tap + SEQ]
                        w = convw_sb[:, h, tap:tap + 1]
                        if tap == KCONV - 1:
                            ins = v_.tensor_scalar(conv[:, h, :], src, w, None, ALU.mult)
                        else:
                            ins = v_.scalar_tensor_tensor(conv[:, h, :], src, w, conv[:, h, :], ALU.mult, ALU.add)
                        if tap:
                            chain.add(ins)
                        else:
                            ins.then_inc(conv_ready, 1)
                    if tap:
                        chain.wait()
                dve.wait_ge(b3_high, b + 1)
                v_.tensor_tensor(b3_rest[:, :], ps[0:B3, 0:2, :].rearrange("p a t -> p (a t)"), b3[:, :], ALU.subtract)\
                    .then_inc(b3_rest_ready, 1)
                dve.wait_ge(b3_mid_ready, 2 * b + 2)
                v_.tensor_tensor(b3[64:96, :], b3_rest[64:96, :], b3_mid[64:96, :], ALU.subtract).then_inc(b3_ready, 1)
                for h in range(EH):
                    dve.wait_ge(e_ready, 2 * EH * b + 2 * h + 1)
                    val = ps[:, 4 + 2 * h:6 + 2 * h, :].rearrange("p a t -> p (a t)")
                    v_.tensor_scalar(delta[:, h, :], val, bdt_sb[:, h:h + 1], 0.0, ALU.add, ALU.max).then_inc(relu_part, 1)
                for h in range(EH):
                    dve.wait_ge(s2_ready, EH * b + h + 1)
                for step in range(5):
                    for h in range(EH):
                        p = conv[:, h, :]
                        if step == 0:
                            chain.add(v_.tensor_scalar(p, s2buf[:, h, :], ATANH[4], ATANH[3], ALU.mult, ALU.add))
                        elif step == 1:
                            chain.add(v_.tensor_tensor(p, p, s2buf[:, h, :], ALU.mult))
                        elif step < 4:
                            chain.add(v_.scalar_tensor_tensor(p, p, ATANH[4 - step], s2buf[:, h, :], ALU.add, ALU.mult))
                        else:
                            v_.scalar_tensor_tensor(s2buf[:, h, :], p, ATANH[0], sbuf_[:, h, :], ALU.add, ALU.mult)\
                                .then_inc(log1p_ready, 1)
                    if step < 4:
                        chain.wait()
                dve.wait_ge(du_ready, EH * b + EH)
                for c in range(NCH):
                    q = b * NCH + c
                    dbu_step(c, 0, 0, q)
                    scan_pair(q, c, 0, False)
                    with dve.Fori(1, NST // 2 - 1) as i:
                        scan_pair(q, c, i, False)
                    scan_pair(q, c, NST // 2 - 1, True)
                    dve.wait_ge(y_added, STEPS * (q + 1))
                    dve.wait_ge(z_ready, 4 * (b + 1))
                    for h in range(EH):
                        v_.scalar_tensor_tensor(y2[:, h, :], u[:, h, c * CH:(c + 1) * CH], dpar_sb[:, h:h + 1], ps[:, 4 + h, :],
                                                ALU.mult, ALU.add).then_inc(y_read, 1)
                    for h in range(EH):
                        dve.wait_ge(y_read, EH * q + h + 1)
                        v_.tensor_tensor(y2[:, h, :], y2[:, h, :], zs[:, h, c * CH:(c + 1) * CH], ALU.mult).then_inc(y2_ready, 1)
                    dve.wait_ge(mamba_out, q + 1)
                    dve.wait_ge(resid_added, 3 * b + 1)
                    xs = x_of(b)[:, TPC * c:TPC * (c + 1), :].rearrange("p t d -> p (t d)")
                    chain.link(v_.tensor_tensor(xs, ps[:, 6, :], xs, ALU.add))
                layer_norm(b, m, False)
                ffn(b, 2 * b, l + 1)
                layer_norm(b, m + 1, False)
                attention(b)
                layer_norm(b, m + 2, False)
                ffn(b, 2 * b + 1, l + 3)
                m += 3
                v_.engine_nop().then_inc(x_final, 1)

        @block.tensor
        def _(pe):
            mm = nc.tensor.matmul

            def xT(l):
                for t in range(2):
                    pe.wait_ge(xn_ready, 2 * l + t + 1)
                    for i in range(4):
                        ins = nc.tensor.transpose(ps[:, t, i * P:(i + 1) * P], xn[:, 4 * t + i, :], ident[:, :])
                    ins.then_inc(xT_in_psum, 1)

            def b_row(q, c, i, par):
                n = i * 2 + par
                if not (q == 0 and isinstance(i, int) and i == 0):
                    pe.wait_ge(dbu_ready, i * 4 + (q * STEPS + 2 * par - 2))
                mm(ps[:, 2 + par, :], bsel[:, bass.ds(n, 1), :].rearrange("p o m -> p (o m)"),
                   b3[:, c * CH:(c + 1) * CH], start=True, stop=True).then_inc(B_ready, 1)

            def y_sum(q, i, par, first, last):
                for h in range(EH):
                    j = par * EH + h
                    pe.wait_ge(prod_ready, i * 4 + (q * STEPS + j + 1))
                    mm(ps[:, 4 + h, :], ident[:, :], prod[:, j, :], start=first and par == 0, stop=last and par == 1)\
                        .then_inc(y_added, 1)

            def ffn(idx, l):
                def up(v):
                    U = idx * 8 + v
                    f, t = v % FC, v // FC
                    if v >= 2:
                        pe.wait_ge(hid_ready, U - 1)
                    if v % FC == 0:
                        pe.wait_ge(xnT_ready, 2 * l + t + 1)
                    mm(ps[:, 2 + v % 2, :], w1_v[:, f, :], xnT[:, t * CH:(t + 1) * CH], start=True, stop=True).then_inc(hid_in_psum, 1)

                def down(v):
                    U = idx * 8 + v
                    f, t = v % FC, v // FC
                    pe.wait_ge(act_ready, U + 1)
                    for i in range(TPC):
                        ins = mm(ps[:, 4 + t, i * D:(i + 1) * D], act_sb[:, U % SLOTS, i * P:(i + 1) * P], w2_sb[:, f, :],
                                 start=(f == 0 and i == 0), stop=(f == FC - 1), skip_group_check=True)
                    ins.then_inc(act_used, 1)

                for v in range(8 + 2):
                    if v < 8:
                        up(v)
                    if v >= 2:
                        down(v - 2)

            def attention(b, l):
                pe.wait_ge(xnT_ready, 2 * l + 2)
                for w, bank in ((wq_sb, 2), (wk_sb, 4)):
                    for t in range(2):
                        mm(ps[:, bank + t, :], w[:, :], xnT[:, t * CH:(t + 1) * CH], start=True, stop=True).then_inc(qkv_in_psum, 1)
                for t in range(2):
                    for i in range(4):
                        ins = mm(ps[:, 6 + t, i * D:(i + 1) * D], xnT[:, (4 * t + i) * P:(4 * t + i + 1) * P], wv_sb[:, :],
                                 start=True, stop=True, skip_group_check=True)
                    ins.then_inc(qkv_in_psum, 1)
                pe.wait_ge(qv_ready, 4 * b + 4)
                pe.wait_ge(k_ready, 2 * b + 2)

                def scores(i, par, first):
                    J = i * 2 + (b * TILES + par)
                    if not first:
                        pe.wait_ge(probs_ready, J - 1)
                    kt = kT[:, (2 * i + par) * P:(2 * i + par + 1) * P]
                    for t in range(2):
                        ins = mm(ps[:, 2 * par + t, :], kt, qT[:, t * CH:(t + 1) * CH], start=True, stop=True)
                    ins.then_inc(scores_ready, 1)

                def turn(i, par):
                    J = i * 2 + (b * TILES + par)
                    pe.wait_ge(probs_ready, J + 1)
                    for t in range(2):
                        if not (b == 0 and isinstance(i, int) and i == 0 and par == 0):
                            pe.wait_ge(pT_act if t == 0 else pT_dve, J)
                        for s in range(4):
                            ins = nc.tensor.transpose(ps[:, 4 + t, s * P:(s + 1) * P], pm[:, par, (4 * t + s) * P:(4 * t + s + 1) * P], ident[:, :])
                        ins.then_inc(pT_in_psum, 1)

                def p_v(i, par, first):
                    J = i * 2 + (b * TILES + par)
                    pe.wait_ge(pT_act, J + 1)
                    pe.wait_ge(pT_dve, J + 1)
                    if not first:
                        pe.wait_ge(attn_added, J - 1)
                    for s in range(TILES):
                        ins = mm(ps[:, 6 + par, 0:D], pT[:, par, s, :], vt[:, s, :], start=(s == 0), stop=(s == TILES - 1))
                    ins.then_inc(attn_out, 1)

                scores(0, 0, b == 0)
                scores(0, 1, b == 0)
                turn(0, 0)
                p_v(0, 0, b == 0)
                turn(0, 1)
                for i in range(1, TILES // 2):
                    scores(i, 0, False)
                    p_v(i - 1, 1, b == 0)
                    turn(i, 0)
                    scores(i, 1, False)
                    p_v(i, 0, False)
                    turn(i, 1)
                p_v(TILES // 2 - 1, 1, False)

            pe.wait_ge(consts_made, 3)
            pe.wait_ge(mamba_w_loaded, 16 * N_MAMBA)
            pe.wait_ge(win_scaled, 1)
            for b in range(BATCH):
                l = 4 * b
                xT(l)
                for s in range(2):
                    for h in range(EH):
                        for t in range(2):
                            if s == 0 and h == 0:
                                pe.wait_ge(xnT_ready, 2 * l + t + 1)
                            mm(ps[:, (2 + 4 * s + 2 * h + t) % 8, :], win_v[:, s, h, :], xnT[:, t * CH:(t + 1) * CH],
                               start=True, stop=True).then_inc(inproj_done, 1)
                pe.wait_ge(u_ready, EH * (b + 1))
                for t in range(2):
                    for h in range(EH):
                        ins = mm(ps[0:RANK + 2 * NST, 2 + t, :], wx_sb[:, h, :], u[:, h, t * CH:(t + 1) * CH],
                                 start=(h == 0), stop=(h == EH - 1))
                    ins.then_inc(xdb_in_psum, 1)
                if b == 0:
                    pe.wait_ge(wb3_ready, 1)
                for t in range(2):
                    for h in range(EH):
                        ins = mm(ps[0:B3, t, :], wb3_sb[:, h, :], u[:, h, t * CH:(t + 1) * CH],
                                 start=(h == 0), stop=(h == EH - 1))
                ins.then_inc(b3_in_psum, 1)
                for h in range(EH):
                    for t in range(2):
                        if h == 0:
                            pe.wait_ge(xdb_ready, 2 * b + t + 1)
                        mm(ps[:, 4 + 2 * h + t, :], wdt_v[:, h, :], xdb[0:RANK, t * CH:(t + 1) * CH],
                           start=True, stop=True).then_inc(dt_in_psum, 1)
                pe.wait_ge(relu_part, EH * (b + 1))
                pe.wait_ge(e_ready, 2 * EH * (b + 1))
                pe.wait_ge(b3_ready, b + 1)
                for c in range(NCH):
                    q = b * NCH + c
                    if q:
                        pe.wait_ge(y_read, EH * q)
                    b_row(q, c, 0, 0)
                    b_row(q, c, 0, 1)
                    y_sum(q, 0, 0, True, False)
                    b_row(q, c, 1, 0)
                    y_sum(q, 0, 1, False, False)
                    b_row(q, c, 1, 1)
                    with pe.Fori(1, NST // 2 - 1) as i:
                        y_sum(q, i, 0, False, False)
                        b_row(q, c, i + 1, 0)
                        y_sum(q, i, 1, False, False)
                        b_row(q, c, i + 1, 1)
                    y_sum(q, NST // 2 - 1, 0, False, False)
                    y_sum(q, NST // 2 - 1, 1, False, True)
                    pe.wait_ge(y2_ready, EH * (q + 1))
                    for i in range(TPC):
                        for h in range(EH):
                            ins = mm(ps[:, 6, i * D:(i + 1) * D], y2[:, h, i * P:(i + 1) * P], wout_sb[:, h, :],
                                     start=(h == 0), stop=(h == EH - 1), skip_group_check=True)
                    ins.then_inc(mamba_out, 1)
                if b == 0:
                    pe.wait_ge(late_w_loaded, 16 * N_LATE)
                xT(l + 1)
                ffn(2 * b, l + 1)
                xT(l + 2)
                attention(b, l + 2)
                xT(l + 3)
                ffn(2 * b + 1, l + 3)


_INS = ['L0_attn_a_hidden_states', 'L0_attn_a_norm_w', 'L0_attn_a_W_in', 'L0_attn_a_conv_w', 'L0_attn_a_W_x',
        'L0_attn_a_W_dt', 'L0_attn_a_b_dt', 'L0_attn_a_A_log', 'L0_attn_a_D_param', 'L0_attn_a_W_out',
        'L0_attn_b_W_query', 'L0_attn_b_W_key', 'L0_attn_b_W_value', 'L0_ffn_W1', 'L0_ffn_b1',
        'L0_ffn_quantum_phases', 'L0_ffn_quantum_weights_real', 'L0_ffn_quantum_weights_imag', 'L0_ffn_W2', 'L0_ffn_b2']
_OUTS = [((BATCH, SEQ, D), 'float32')]


def kernel(**inputs):
    import concourse.bacc as _bacc
    from concourse.bass_utils import run_bass_kernel_spmd as _run

    nc = _bacc.Bacc("TRN2", target_bir_lowering=False, num_devices=1)
    arrays, args = {}, []
    for name in _INS:
        a = np.ascontiguousarray(inputs[name])
        arrays[f"in_{name}_dram"] = a
        args.append(nc.dram_tensor(f"in_{name}_dram", a.shape, mybir.dt.from_np(a.dtype), kind="ExternalInput").ap())
    for i, (shape, dtype) in enumerate(_OUTS):
        args.append(nc.dram_tensor(f"out_{i}_dram", shape, mybir.dt.from_np(np.dtype(dtype)), kind="ExternalOutput").ap())
    build(nc, *args)
    r = _run(nc, [arrays], core_ids=[0])
    return tuple(r.results[0][f"out_{i}_dram"] for i in range(len(_OUTS)))[0]
```

```python
from contextlib import ExitStack

import numpy as np

import concourse.bass as bass
from concourse import mybir

ALU = mybir.AluOpType
ACT = mybir.ActivationFunctionType
AX_X = mybir.AxisListType.X
F32 = mybir.dt.float32
BF16 = mybir.dt.bfloat16

P = 128
BATCH, SEQ, D = 2, 1024, 128
TILES = SEQ // P
E, NST, RANK, KCONV = 256, 16, 64, 4
EH = E // P
F = 512
FC = F // P
CH = 512
NCH = SEQ // CH
TPC = CH // P
B3 = 96
SLOTS = 4
STEPS = NST * EH
NPT = 4
QK = float(1.0 / np.sqrt(D))
LN_EPS, RMS_EPS = 1e-5, 1e-6

ROUND = 1.5 * 2.0 ** 23
TWO_PI = 2.0 * np.pi
INV_2PI = float(np.float32(1.0 / TWO_PI))
C1 = 6.28125
C2 = float(np.round((TWO_PI - C1) * 2.0 ** 20) / 2.0 ** 20)
C3 = float(TWO_PI - C1 - C2)
PI_LO = float(np.nextafter(np.float32(np.pi), np.float32(0)))
ATANH = (2.0000000076817575, 0.6666632164139702, 0.4002459522991947, 0.27965157756134756, 0.28157778314218707)

DA, BB, YY, SIDE = 0, 2, 3, 5
SIDE_USES = (
    [(s, 0, n) for s, n in (("norm1", 2), ("x0", 2), ("x1", 2), ("z0", 2), ("z1", 2), ("xdb", 2), ("b3", 2), ("dt0", 2), ("dt1", 2))]
    + [(s, 1, n) for s, n in (("norm1", 2), ("x0", 2), ("x1", 2), ("z0", 2), ("z1", 2))]
    + [("out", 0, 1)]
    + [(s, 1, n) for s, n in (("xdb", 2), ("b3", 2), ("dt0", 2), ("dt1", 2))]
    + [("out", 1, 1), ("norm2", 0, 2), ("norm3", 0, 2), ("qkv", 0, 6), ("out", 2, 1), ("out", 3, 1),
       ("norm4", 0, 2), ("norm2", 1, 2), ("norm3", 1, 2), ("qkv", 1, 6), ("norm4", 1, 2)]
)
FIRST, DONE = {}, {}
_w = 0
for _s, _b, _n in SIDE_USES:
    FIRST[_s, _b] = _w
    _w += _n
    DONE[_s, _b] = _w
NORMS = [("norm1", 0), ("norm1", 1), ("norm2", 0), ("norm3", 0), ("norm4", 0), ("norm2", 1), ("norm3", 1), ("norm4", 1)]
ROOTS = {n: i + min(i, 2) for i, n in enumerate(NORMS)}
FFNS = [("norm2", 0), ("norm4", 0), ("norm2", 1), ("norm4", 1)]
ADDS = [("norm1", 0), ("norm1", 1)] + FFNS


def build(nc, hidden, norm_w, w_in, conv_w, w_x, w_dt, b_dt, a_log, d_param, w_out,
          w_q, w_k, w_v, w1, b1, phases, q_real, q_imag, w2, b2, out):
    with ExitStack() as ctx:
        def sb(name, shape, dt=F32):
            return ctx.enter_context(nc.sbuf_tensor(name, shape, dt))

        def sem(name):
            return ctx.enter_context(nc.semaphore(name))

        x_tok = sb("x_tok", [P, BATCH * TILES, D])
        xn = sb("xn", [P, TILES, D])
        xnT = sb("xnT", [P, BATCH, SEQ])
        win_sb = sb("win_sb", [P, 2 * E])
        wx_sb = sb("wx_sb", [P, EH, RANK + 2 * NST])
        wdt_sb = sb("wdt_sb", [RANK, E])
        wout_sb = sb("wout_sb", [P, EH, D])
        w1_sb = sb("w1_sb", [P, F])
        w2_sb = sb("w2_sb", [P, FC, D])
        wq_sb = sb("wq_sb", [P, D])
        wk_sb = sb("wk_sb", [P, D])
        wv_sb = sb("wv_sb", [P, D])
        normw_sb = sb("normw_sb", [P, 1])
        convw_sb = sb("convw_sb", [P, EH, KCONV])
        bdt_sb = sb("bdt_sb", [P, EH])
        dpar_sb = sb("dpar_sb", [P, EH])
        a_sb = sb("a_sb", [P, EH, NST])
        b1_sb = sb("b1_sb", [P, FC])
        theta = sb("theta", [P, FC])
        wr_sb = sb("wr_sb", [P, FC])
        wi_sb = sb("wi_sb", [P, FC])
        b2_sb = sb("b2_sb", [P, D])
        rho = sb("rho", [P, FC])
        rho_turns = sb("rho_turns", [P, FC])
        trig = sb("trig", [P, 8, FC])
        coef = sb("coef", [P, FC])
        ident = sb("ident", [P, P])
        diag_d = sb("diag_d", [P, EH, P])
        bsel = sb("bsel", [B3, NST, P], BF16)
        wb3_sb = sb("wb3_sb", [P, EH, B3])
        b3 = sb("b3", [B3, BATCH, SEQ], BF16)
        b3_mid = sb("b3_mid", [B3, SEQ], BF16)
        two = sb("two", [P, 1])

        stats = sb("stats", [P, TILES, 6])
        mv = sb("mv", [P, TILES, 2])
        var_eps = sb("var_eps", [P, TILES])
        lnv = sb("lnv", [P, TILES])
        rstd0 = sb("rstd0", [P, TILES])
        newton = sb("newton", [P, TILES])
        rstd = sb("rstd", [P, TILES])
        rstd2 = sb("rstd2", [P, TILES])

        xin = sb("xin", [P, EH, KCONV - 1 + SEQ])
        u = sb("u", [P, BATCH, EH, SEQ])
        zs = sb("zs", [P, BATCH, EH, SEQ])
        delta = sb("delta", [P, BATCH, EH, SEQ])
        du = sb("du", [P, BATCH, EH, SEQ])
        xdb = sb("xdb", [RANK + 2 * NST, SEQ])
        ebuf = sb("ebuf", [P, EH, SEQ])
        sbuf_ = sb("sbuf_", [P, EH, SEQ])
        s2buf = sb("s2buf", [P, EH, SEQ])
        c_all = sb("c_all", [P, NST, CH])
        dbu = sb("dbu", [P, SLOTS, CH])
        hs = sb("hs", [P, SLOTS, CH])
        prod = sb("prod", [P, SLOTS, CH])
        state = sb("state", [P, STEPS])
        y2 = sb("y2", [P, EH, CH])
        kstat = sb("kstat", [P, P])
        rsum = sb("rsum", [P, 2])
        mx = sb("mx", [P, 2])
        negm = sb("negm", [P, 2])
        rinv = sb("rinv", [P, 2])

        def as_slots(t):
            return t.rearrange("p h (s t) -> p (h s) t", t=CH)

        x1 = s2buf[:, 0, :].rearrange("p (i d) -> p i d", d=D)
        b3_full = s2buf[0:B3, 0, :]
        b3_rest = s2buf[0:B3, 1, :]
        hid, tbuf, turn = as_slots(ebuf[:, :, :]), as_slots(sbuf_[:, :, :]), as_slots(s2buf[:, :, :])
        jbuf, sn, act_sb = as_slots(zs[:, 0, :, :]), as_slots(delta[:, 0, :, :]), as_slots(u[:, 0, :, :])
        pm = jbuf[:, :, :].rearrange("p (a s) t -> p a (s t)", a=2)
        pT = sn[:, :, :].rearrange("p (a s) (i d) -> p a (s i) d", a=2, d=P)
        vt = xin[:, 0, KCONV - 1:].rearrange("p (i d) -> p i d", d=D)

        def qT(b):
            return du[:, b, 0, :]

        def kT(b):
            return du[:, b, 1, :]

        c_dram = nc.dram_tensor("c_scratch", [BATCH, NST, SEQ], F32, kind="Internal").ap()
        ps = ctx.enter_context(nc.psum_tensor("ps", [P, 8, CH], F32))

        x_loaded = [sem(f"x_loaded{b}") for b in range(BATCH)]
        mamba_w_loaded = sem("mamba_w_loaded")
        small_w_loaded = sem("small_w_loaded")
        late_w_loaded = sem("late_w_loaded")
        consts_made = sem("consts_made")
        wb3_ready = sem("wb3_ready")
        pool_chain = sem("pool_chain")
        act_chain = sem("act_chain")
        dve_chain = sem("dve_chain")
        win_scaled = sem("win_scaled")
        diag_ready = sem("diag_ready")
        trig_args = sem("trig_args")
        trig_done = sem("trig_done")
        a_exp = sem("a_exp")
        a_ready = sem("a_ready")
        side_filled = sem("side_filled")
        side_copied = sem("side_copied")
        var_ready = sem("var_ready")
        rstd_guess = sem("rstd_guess")
        xn_ready = sem("xn_ready")
        x_added = sem("x_added")
        conv_ready = sem("conv_ready")
        u_ready = sem("u_ready")
        b3_high = sem("b3_high")
        b3_rest_ready = sem("b3_rest_ready")
        b3_mid_ready = sem("b3_mid_ready")
        b3_ready = sem("b3_ready")
        relu_part = sem("relu_part")
        e_ready = sem("e_ready")
        s_ready = sem("s_ready")
        s2_ready = sem("s2_ready")
        du_ready = sem("du_ready")
        c_stored = sem("c_stored")
        c_loaded = sem("c_loaded")
        dA_ready = sem("dA_ready")
        B_ready = sem("B_ready")
        dbu_ready = sem("dbu_ready")
        h_ready = sem("h_ready")
        prod_ready = sem("prod_ready")
        y_added = sem("y_added")
        y2_ready = sem("y2_ready")
        hid_in_psum = sem("hid_in_psum")
        hid_ready = sem("hid_ready")
        sum_ready = sem("sum_ready")
        part_ready = sem("part_ready")
        turns_ready = sem("turns_ready")
        arg_ready = sem("arg_ready")
        whole_ready = sem("whole_ready")
        sin_ready = sem("sin_ready")
        q_ready = sem("q_ready")
        act_ready = sem("act_ready")
        act_used = sem("act_used")
        out_read = sem("out_read")
        kstat_ready = sem("kstat_ready")
        scores_ready = sem("scores_ready")
        mx_ready = sem("mx_ready")
        negm_ready = sem("negm_ready")
        probs_ready = sem("probs_ready")
        rinv_ready = sem("rinv_ready")
        pT_in_psum = sem("pT_in_psum")
        pT_low = sem("pT_low")
        pT_high = sem("pT_high")
        attn_out = sem("attn_out")
        attn_added = sem("attn_added")
        x_final = sem("x_final")
        stored = sem("stored")

        class Chain:
            def __init__(self, eng, s):
                self.eng, self.s, self.n = eng, s, 0

            def add(self, ins):
                ins.then_inc(self.s, 1)
                self.n += 1

            def wait(self):
                self.eng.wait_ge(self.s, self.n)

            def link(self, ins):
                self.add(ins)
                self.wait()

        def is0(v):
            return isinstance(v, int) and v == 0

        x_dram = hidden.rearrange("b (t p) d -> b p t d", p=P)
        out_dram = out.rearrange("b (t p) d -> b p t d", p=P)

        def x_of(b):
            return x_tok[:, b * TILES:(b + 1) * TILES, :]

        def flat(ap):
            return ap.rearrange("p a t -> p (a t)")

        win_v = win_sb[:, :].rearrange("k (s p c) -> k s c p", s=2, c=EH)
        wdt_v = wdt_sb[:, :].rearrange("k (p c) -> k c p", c=EH)
        w1_v = w1_sb[:, :].rearrange("k (p c) -> k c p", c=FC)
        N_SMALL, N_MAMBA, N_LATE = 5, 5, 9

        block = ctx.enter_context(nc.Block())

        @block.sync
        def _(sp):
            sp.dma_start(x_of(0), x_dram[0]).then_inc(x_loaded[0], 16)
            sp.dma_start(win_sb[:, :], w_in).then_inc(mamba_w_loaded, 16)
            sp.dma_start(normw_sb[:, :], norm_w.rearrange("(p o) -> p o", o=1)).then_inc(mamba_w_loaded, 16)
            sp.dma_start(wx_sb[:, :, :], w_x.rearrange("(p c) r -> p c r", c=EH)).then_inc(mamba_w_loaded, 16)
            sp.dma_start(wdt_sb[:, :], w_dt).then_inc(mamba_w_loaded, 16)
            sp.dma_start(wout_sb[:, :, :], w_out.rearrange("(p c) d -> p c d", c=EH)).then_inc(mamba_w_loaded, 16)
            sp.dma_start(convw_sb[:, :, :], conv_w.rearrange("(p c) o k -> p c (o k)", c=EH)).then_inc(small_w_loaded, 16)
            sp.dma_start(a_sb[:, :, :], a_log.rearrange("(p c) n -> p c n", c=EH)).then_inc(small_w_loaded, 16)
            sp.dma_start(bdt_sb[:, :], b_dt.rearrange("(p c) -> p c", c=EH)).then_inc(small_w_loaded, 16)
            sp.dma_start(dpar_sb[:, :], d_param.rearrange("(p c) -> p c", c=EH)).then_inc(small_w_loaded, 16)
            sp.dma_start(theta[:, :], phases.rearrange("(p c) -> p c", c=FC)).then_inc(small_w_loaded, 16)
            sp.dma_start(x_of(1), x_dram[1]).then_inc(x_loaded[1], 16)
            for dst, src in ((b1_sb, b1), (wr_sb, q_real), (wi_sb, q_imag)):
                sp.dma_start(dst[:, :], src.rearrange("(p c) -> p c", c=FC)).then_inc(late_w_loaded, 16)
            sp.dma_start(b2_sb[:, :], b2.partition_broadcast(P)).then_inc(late_w_loaded, 16)
            sp.dma_start(w1_sb[:, :], w1).then_inc(late_w_loaded, 16)
            sp.dma_start(w2_sb[:, :, :], w2.rearrange("(p c) d -> p c d", c=FC)).then_inc(late_w_loaded, 16)
            for dst, src in ((wq_sb, w_q), (wk_sb, w_k), (wv_sb, w_v)):
                sp.dma_start(dst[:, :], src).then_inc(late_w_loaded, 16)

            def store_c(b):
                sp.wait_ge(side_copied, DONE["xdb", b])
                sp.dma_start(c_dram[b], xdb[RANK + NST:RANK + 2 * NST, :]).then_inc(c_stored, 16)
                sp.wait_ge(c_stored, 16 * (b + 1))

            for q in range(BATCH * NCH):
                b, c = q // NCH, q % NCH
                if c == 0:
                    store_c(b)
                for g in range(NST // 2):
                    if q:
                        sp.wait_ge(prod_ready, STEPS * (q - 1) + 4 * (g + 1))
                    src = c_dram[b, 2 * g:2 * g + 2, c * CH:(c + 1) * CH].partition_broadcast(P)
                    sp.dma_start(c_all[:, 2 * g:2 * g + 2, :], src).then_inc(c_loaded, 16)
                    sp.wait_ge(c_loaded, 16 * (q * NST // 2 + g + 1))
            for b in range(BATCH):
                sp.wait_ge(x_final, b + 1)
                sp.dma_start(out_dram[b], x_of(b)).then_inc(stored, 16)
            sp.wait_ge(stored, 16 * BATCH)

        @block.gpsimd
        def _(pool):
            chain = Chain(pool, pool_chain)
            g = nc.gpsimd
            g.memset(two[:, :], 2.0).then_inc(consts_made, 1)
            chain.link(g.memset(ident[:, :], 0.0))
            g.affine_select(out=ident[:, :], in_=ident[:, :], compare_op=ALU.not_equal, fill=1.0, base=0,
                            pattern=[[-1, P]], channel_multiplier=1).then_inc(consts_made, 1)
            chain.link(g.memset(wb3_sb[:, :, :], 0.0))
            pool.wait_ge(mamba_w_loaded, 16 * N_MAMBA)
            for part in range(3):
                ins = g.tensor_copy(wb3_sb[:, :, 32 * part:32 * part + NST], wx_sb[:, :, RANK:RANK + NST])
            ins.then_inc(wb3_ready, 1)
            chain.link(g.memset(bsel[:, :, :], 0.0))
            for part in range(3):
                ins = g.affine_select(out=bsel[:, :, :], in_=bsel[:, :, :], compare_op=ALU.not_equal, fill=1.0,
                                      base=-32 * part, pattern=[[-1, NST], [0, P]], channel_multiplier=1)
                if part < 2:
                    chain.link(ins)
            ins.then_inc(consts_made, 1)

            def products(q, i, r):
                k = i * (2 * NPT) + (q * STEPS + 2 * r)
                c_row = flat(c_all[:, bass.ds(i * NPT + r, 1), :])
                for h in range(EH):
                    if h == 0 and r % 2 == 0:
                        pool.wait_ge(c_loaded, i * 32 + (16 * (q * NST // 2 + r // 2 + 1)))
                    pool.wait_ge(h_ready, k + (h + 1))
                    if not (q == 0 and is0(i) and r < 2):
                        pool.wait_ge(y_added, k + (h + 1 - SLOTS))
                    if not isinstance(i, int):
                        pool.nop(nofuse=True)
                    sl = (2 * r + h) % SLOTS
                    g.tensor_tensor(prod[:, sl, :], hs[:, sl, :], c_row, ALU.mult).then_inc(prod_ready, 1)

            def key_tile(J, col, first):
                if not first:
                    pool.wait_ge(scores_ready, J)
                if not isinstance(J, int):
                    pool.nop(nofuse=True)
                g.tensor_copy(kstat[:, :], kT(0)[:, bass.ds(col, P)]).then_inc(kstat_ready, 1)

            def add_bias(norm):
                pool.wait_ge(xn_ready, 2 * NORMS.index(norm) + 2)
                b = norm[1]
                g.tensor_tensor(x_of(b), x_of(b), b2_sb[:, :].unsqueeze(1).to_broadcast([P, TILES, D]), ALU.add)\
                    .then_inc(x_added, 1)

            def ffn(ffns):
                for norm in ffns:
                    for v in range(8):
                        U = 8 * FFNS.index(norm) + v
                        sl = U % SLOTS
                        pool.wait_ge(whole_ready, U + 1)
                        g.tensor_tensor(jbuf[:, sl, :], turn[:, sl, :], jbuf[:, sl, :], ALU.subtract).then_inc(part_ready, 1)

            def add_ln(b):
                pool.wait_ge(xn_ready, 2 * b + 2)
                g.tensor_tensor(x_of(b), x_of(b), x1, ALU.add).then_inc(x_added, 1)

            add_ln(0)
            for q in range(NCH):
                for n in range(NST):
                    products(q, n // NPT, n % NPT)
                    if q == 0 and n == 6:
                        add_ln(1)
            add_bias(FFNS[0])
            ffn(FFNS[0:1])
            pool.wait_ge(side_copied, DONE["qkv", 0])
            key_tile(0, 0, True)
            for q in range(NCH, 2 * NCH):
                def tile(i, first):
                    J = i + (q - NCH) * NPT
                    for r in range(NPT):
                        products(q, i, r)
                        if r == 1 and not (q == 2 * NCH - 1 and first == "last"):
                            key_tile(J + 1, i * P + ((q - NCH) * NPT * P + P), False)
                tile(0, "first")
                with pool.Fori(1, NST // NPT - 1) as i:
                    tile(i, "")
                tile(NST // NPT - 1, "last")
            add_bias(FFNS[1])
            add_bias(FFNS[2])
            ffn(FFNS[1:3])
            add_bias(FFNS[3])
            ffn(FFNS[3:4])

        @block.scalar
        def _(act):
            chain = Chain(act, act_chain)
            s = nc.scalar

            def exp_tables():
                s.preload_act_table_set("natural_log_exp_and_others")

            def silu_sin_tables():
                s.preload_act_table_set("silu_and_others")

            def root(m):
                act.wait_ge(var_ready, m + 1)
                chain.link(s.activation(lnv[:, :], var_eps[:, :], ACT.Ln))
                s.activation(rstd0[:, :], lnv[:, :], ACT.Exp, scale=-0.5).then_inc(rstd_guess, 1)

            def copy_out(use, dsts, rows=P, bias=None):
                for t, dst in enumerate(dsts):
                    w = FIRST[use] + t
                    act.wait_ge(side_filled, w + 1)
                    src = ps[0:rows, SIDE + w % 3, :]
                    if bias is None:
                        s.copy(dst, src).then_inc(side_copied, 1)
                    else:
                        s.activation(dst, src, ACT.Identity, bias=bias).then_inc(side_copied, 1)

            def halves(ap):
                return [ap[:, t * CH:(t + 1) * CH] for t in range(2)]

            def norm_copies(norm):
                copy_out(norm, halves(xnT[:, norm[1], :]))

            def mamba_in(b, p):
                if p == 1:
                    root(ROOTS["norm1", b])
                elif p == 3:
                    root(ROOTS["norm1", b] + 1)
                elif p == 6:
                    norm_copies(("norm1", b))
                elif p in (8, 10):
                    h = (p - 8) // 2
                    copy_out((f"x{h}", b), halves(xin[:, h, KCONV - 1:]))
                elif p in (12, 14):
                    h = (p - 12) // 2
                    copy_out((f"z{h}", b), halves(zs[:, b, h, :]))
                elif p == 15:
                    silu_sin_tables()
                    act.wait_ge(side_copied, DONE["z1", b])
                    chain.add(s.activation(zs[:, b, :, :], zs[:, b, :, :], ACT.Silu))
                    act.wait_ge(conv_ready, b + 1)
                    s.activation(u[:, b, :, :], u[:, b, :, :], ACT.Silu).then_inc(u_ready, 1)
                    exp_tables()
                elif p == 17:
                    copy_out(("xdb", b), halves(xdb[:, :]), rows=RANK + 2 * NST)
                elif p == 19:
                    act.wait_ge(x_added, b + 1)
                    copy_out(("b3", b), halves(b3_full), rows=B3)
                elif p == 20:
                    act.wait_ge(side_copied, DONE["b3", b])
                    s.copy(b3[:, b, :], b3_full).then_inc(b3_high, 1)
                elif p in (21, 23):
                    h = (p - 21) // 2
                    copy_out((f"dt{h}", b), halves(ebuf[:, h, :]), bias=bdt_sb[:, h:h + 1])
                elif p == 22:
                    act.wait_ge(b3_rest_ready, b + 1)
                    s.copy(b3[32:64, b, :], b3_rest[32:64, :]).then_inc(b3_mid_ready, 1)
                    s.copy(b3_mid[64:96, :], b3_rest[64:96, :]).then_inc(b3_mid_ready, 1)
                elif p == 24:
                    act.wait_ge(side_copied, DONE["dt1", b])
                    chain.add(s.activation(sbuf_[:, :, :], ebuf[:, :, :], ACT.Abs))
                elif p == 25:
                    chain.wait()
                    act.wait_ge(relu_part, b + 1)
                    chain.add(s.activation(ebuf[:, :, :], sbuf_[:, :, :], ACT.Exp, scale=-1.0))
                elif p == 26:
                    chain.wait()
                    chain.add(s.activation(sbuf_[:, :, :], ebuf[:, :, :], ACT.Ln, bias=two[:, :]))
                elif p == 27:
                    chain.wait()
                    s.activation(sbuf_[:, :, :], sbuf_[:, :, :], ACT.Exp, scale=-1.0).then_inc(e_ready, 1)
                elif p == 29:
                    act.wait_ge(s_ready, b + 1)
                    s.activation(s2buf[:, :, :], sbuf_[:, :, :], ACT.Square).then_inc(s2_ready, 1)

            def decays(q, i, r):
                b, c = q // NCH, q % NCH
                k = i * (2 * NPT) + (q * STEPS + 2 * r)
                for h in range(EH):
                    if not (q == 0 and is0(i) and r == 0):
                        act.wait_ge(h_ready, k + (h - 1))
                    s.activation(ps[:, DA + h, :], delta[:, b, h, c * CH:(c + 1) * CH], ACT.Exp,
                                 scale=a_sb[:, h, bass.ds(i * NPT + r, 1)]).then_inc(dA_ready, 1)
                    if c == 0 and not (is0(i) and r == 0):
                        sl = (2 * r + h - 2) % SLOTS
                        s.copy(state[:, bass.ds(i * (2 * NPT) + (2 * r + h - 2), 1)], hs[:, sl, CH - 1:CH])

            def last_states(q):
                for j in range(STEPS - 2, STEPS):
                    act.wait_ge(h_ready, q * STEPS + j + 1)
                    chain.add(s.copy(state[:, j:j + 1], hs[:, j % SLOTS, CH - 1:CH]))

            def mamba_out(q):
                copy_out(("out", q), [y2[:, 0, :]])

            def ffn(ffns):
                units = [(norm, v) for norm in ffns for v in range(8)]
                silu_sin_tables()

                def evict(norm, v):
                    U = 8 * FFNS.index(norm) + v
                    act.wait_ge(hid_in_psum, U + 1)
                    if U >= SLOTS:
                        act.wait_ge(q_ready, U - SLOTS + 1)
                    s.activation(hid[:, U % SLOTS, :], ps[:, 5 + v % 2, :], ACT.Identity,
                                 bias=b1_sb[:, v % FC:v % FC + 1]).then_inc(hid_ready, 1)

                def turns(norm, v):
                    U = 8 * FFNS.index(norm) + v
                    act.wait_ge(arg_ready, U + 1)
                    s.activation(turn[:, U % SLOTS, :], tbuf[:, U % SLOTS, :], ACT.Identity, bias=rho_turns[:, v % FC:v % FC + 1],
                                 scale=INV_2PI).then_inc(turns_ready, 1)

                def sine(norm, v):
                    U = 8 * FFNS.index(norm) + v
                    act.wait_ge(part_ready, U + 1)
                    s.activation(sn[:, U % SLOTS, :], jbuf[:, U % SLOTS, :], ACT.Sin, scale=2 * PI_LO).then_inc(sin_ready, 1)

                def relu(norm, v):
                    U = 8 * FFNS.index(norm) + v
                    act.wait_ge(q_ready, U + 1)
                    s.activation(act_sb[:, U % SLOTS, :], act_sb[:, U % SLOTS, :], ACT.Relu).then_inc(act_ready, 1)

                for n in range(len(units) + 3):
                    if n < len(units):
                        evict(*units[n])
                    if n >= 1 and n - 1 < len(units):
                        turns(*units[n - 1])
                    if n >= 2 and n - 2 < len(units):
                        sine(*units[n - 2])
                    if n >= 3:
                        relu(*units[n - 3])
                exp_tables()

            def qkv_copies(b):
                copy_out(("qkv", b), halves(qT(b)) + halves(kT(b)) + [flat(vt[:, 4 * t:4 * t + 4, :]) for t in range(2)])

            def probabilities(J, par, bank, reuse):
                act.wait_ge(negm_ready, J + 1)
                if reuse:
                    act.wait_ge(pT_in_psum, (J - reuse) * 2 + 2)
                    act.wait_ge(rinv_ready, J - reuse + 1)
                s.activation(pm[:, par, :], flat(ps[:, bank:bank + 2, :]), ACT.Exp, bias=negm[:, par:par + 1],
                             scale=QK, accum_out=rsum[:, par:par + 1]).then_inc(probs_ready, 1)

            def pT_copy(J, par, low, high, reuse):
                act.wait_ge(pT_in_psum, J * 2 + 1)
                if reuse:
                    act.wait_ge(attn_out, J - reuse + 1)
                s.copy(flat(pT[:, par, 0:4, :]), ps[:, low, :]).then_inc(pT_low, 1)
                if high is not None:
                    act.wait_ge(pT_in_psum, J * 2 + 2)
                    s.copy(flat(pT[:, par, 4:8, :]), ps[:, high, :]).then_inc(pT_high, 1)

            silu_sin_tables()
            act.wait_ge(trig_args, 1)
            s.activation(trig[:, 4:6, :], trig[:, 0:2, :], ACT.Sin).then_inc(trig_done, 1)
            exp_tables()
            act.wait_ge(small_w_loaded, 16 * N_SMALL)
            s.activation(a_sb[:, :, :], a_sb[:, :, :], ACT.Exp).then_inc(a_exp, 1)
            act.wait_ge(consts_made, 3)
            for p in range(30):
                mamba_in(0, p)
            act.wait_ge(a_ready, 1)
            act.wait_ge(du_ready, 1)
            for q in range(NCH):
                for n in range(NST):
                    decays(q, n // NPT, n % NPT)
                    mamba_in(1, NST * q + n)
                if q == 0:
                    last_states(q)
                    mamba_out(q)
            mamba_out(1)
            root(ROOTS[FFNS[0]])
            norm_copies(FFNS[0])
            ffn(FFNS[0:1])
            root(ROOTS["norm3", 0])
            norm_copies(("norm3", 0))
            qkv_copies(0)
            act.wait_ge(du_ready, 2)
            for q in range(NCH, 2 * NCH):
                def tile(i, first):
                    J = i + (q - NCH) * NPT
                    for r in range(NPT):
                        if r == 2:
                            probabilities(J, 0, SIDE, 0 if first else 1)
                        decays(q, i, r)
                        if r == 3:
                            pT_copy(J, 0, SIDE, SIDE + 1, 0 if first else 1)
                tile(0, q == NCH)
                with act.Fori(1, NST // NPT) as i:
                    tile(i, False)
                if q == NCH:
                    last_states(q)
                mamba_out(q)
            root(ROOTS["norm4", 0])
            norm_copies(("norm4", 0))
            root(ROOTS["norm2", 1])
            norm_copies(("norm2", 1))
            ffn(FFNS[1:3])
            root(ROOTS["norm3", 1])
            norm_copies(("norm3", 1))
            qkv_copies(1)
            for par in range(2):
                probabilities(TILES + par, par, 2 * par, 2)
            with act.Fori(0, TILES // 2 - 1) as i:
                for par in range(2):
                    J = i * 2 + (TILES + par)
                    pT_copy(J, par, 4, None, 2)
                    probabilities(J + 2, par, 2 * par, 2)
            for par in range(2):
                pT_copy(2 * TILES - 2 + par, par, 4, None, 2)
            root(ROOTS["norm4", 1])
            norm_copies(("norm4", 1))
            ffn(FFNS[3:4])

        @block.vector
        def _(dve):
            chain = Chain(dve, dve_chain)
            v_ = nc.vector

            def newton_step(m, dst):
                dve.wait_ge(rstd_guess, m + 1)
                chain.link(v_.tensor_tensor(newton[:, :], rstd0[:, :], rstd0[:, :], ALU.mult))
                chain.link(v_.tensor_tensor(newton[:, :], newton[:, :], var_eps[:, :], ALU.mult))
                chain.link(v_.tensor_scalar(newton[:, :], newton[:, :], -0.5, 1.5, ALU.mult, ALU.add))
                chain.link(v_.tensor_tensor(dst[:, :], rstd0[:, :], newton[:, :], ALU.mult))

            def moments(b):
                xb = x_of(b)
                for t in range(TILES):
                    chain.add(v_.bn_stats(stats[:, t, :], xb[:, t, :]))
                chain.wait()
                for t in range(TILES):
                    chain.add(v_.bn_aggr(mv[:, t, :], stats[:, t, :]))
                chain.wait()
                v_.tensor_scalar(var_eps[:, :], mv[:, :, 1], LN_EPS, None, ALU.add).then_inc(var_ready, 1)

            def normalise(b, dst, scale, signal):
                for t in range(TILES):
                    ins = v_.tensor_scalar(dst[:, t, :], x_of(b)[:, t, :], mv[:, t, 0:1], scale[:, t:t + 1],
                                           ALU.subtract, ALU.mult)
                    if signal and t % 4 == 3:
                        ins.then_inc(xn_ready, 1)

            def layer_norm(norm):
                moments(norm[1])
                newton_step(ROOTS[norm], rstd)
                normalise(norm[1], xn, rstd, True)

            def mamba_in(b, p):
                m = ROOTS["norm1", b]
                if p == 0:
                    dve.wait_ge(x_loaded[b], 16)
                    moments(b)
                elif p == 2:
                    newton_step(m, rstd)
                    chain.link(v_.tensor_tensor(newton[:, :], rstd[:, :], rstd[:, :], ALU.mult))
                    chain.link(v_.tensor_tensor(newton[:, :], newton[:, :], mv[:, :, 1], ALU.mult))
                    v_.tensor_scalar(var_eps[:, :], newton[:, :], RMS_EPS, None, ALU.add).then_inc(var_ready, 1)
                elif p == 3:
                    normalise(b, x1, rstd, False)
                elif p == 4:
                    newton_step(m + 1, rstd2)
                    chain.link(v_.tensor_tensor(rstd2[:, :], rstd2[:, :], rstd[:, :], ALU.mult))
                    normalise(b, xn, rstd2, True)
                elif 11 <= p <= 14:
                    tap = 14 - p
                    if tap == KCONV - 1:
                        dve.wait_ge(side_copied, DONE["x1", b])
                    else:
                        chain.wait()
                    for h in range(EH):
                        src = xin[:, h, tap:tap + SEQ]
                        w = convw_sb[:, h, tap:tap + 1]
                        if tap == KCONV - 1:
                            ins = v_.tensor_scalar(u[:, b, h, :], src, w, None, ALU.mult)
                        else:
                            ins = v_.scalar_tensor_tensor(u[:, b, h, :], src, w, u[:, b, h, :], ALU.mult, ALU.add)
                        if tap:
                            chain.add(ins)
                    if not tap:
                        ins.then_inc(conv_ready, 1)
                elif p == 21:
                    dve.wait_ge(b3_high, b + 1)
                    v_.tensor_tensor(b3_rest, b3_full, b3[:, b, :], ALU.subtract).then_inc(b3_rest_ready, 1)
                elif p == 23:
                    dve.wait_ge(b3_mid_ready, 2 * b + 2)
                    v_.tensor_tensor(b3[64:96, b, :], b3_rest[64:96, :], b3_mid[64:96, :], ALU.subtract).then_inc(b3_ready, 1)
                elif p == 24:
                    dve.wait_ge(side_copied, DONE["dt1", b])
                    v_.tensor_scalar(delta[:, b, :, :], ebuf[:, :, :], 0.0, None, ALU.max).then_inc(relu_part, 1)
                elif p == 28:
                    dve.wait_ge(e_ready, b + 1)
                    v_.tensor_tensor(sbuf_[:, :, :], ebuf[:, :, :], sbuf_[:, :, :], ALU.mult).then_inc(s_ready, 1)
                elif p == 30:
                    dve.wait_ge(s2_ready, b + 1)
                    chain.add(v_.tensor_scalar(ebuf[:, :, :], s2buf[:, :, :], ATANH[4], ATANH[3], ALU.mult, ALU.add))
                elif p == 31:
                    chain.wait()
                    chain.add(v_.tensor_tensor(ebuf[:, :, :], ebuf[:, :, :], s2buf[:, :, :], ALU.mult))
                elif p in (32, 33):
                    for h in range(EH):
                        if h == 0:
                            chain.wait()
                        chain.add(v_.scalar_tensor_tensor(ebuf[:, h, :], ebuf[:, h, :], ATANH[34 - p], s2buf[:, h, :], ALU.add, ALU.mult))
                elif p == 34:
                    chain.wait()
                    for h in range(EH):
                        chain.add(v_.scalar_tensor_tensor(ebuf[:, h, :], ebuf[:, h, :], ATANH[0], sbuf_[:, h, :], ALU.add, ALU.mult))
                elif p == 35:
                    chain.wait()
                    chain.add(v_.tensor_tensor(delta[:, b, :, :], delta[:, b, :, :], ebuf[:, :, :], ALU.add))
                elif p == 36:
                    chain.wait()
                    v_.tensor_tensor(du[:, b, :, :], delta[:, b, :, :], u[:, b, :, :], ALU.mult).then_inc(du_ready, 1)

            def drive(q, i, r):
                b, c = q // NCH, q % NCH
                for h in range(EH):
                    if h == 0:
                        dve.wait_ge(B_ready, i * NPT + (q * NST + r + 1))
                    if not (q == 0 and is0(i) and r < 2):
                        dve.wait_ge(h_ready, i * (2 * NPT) + (q * STEPS + 2 * r + h + 1 - SLOTS))
                    v_.tensor_tensor(dbu[:, (2 * r + h) % SLOTS, :], ps[:, BB, :], du[:, b, h, c * CH:(c + 1) * CH], ALU.mult)\
                        .then_inc(dbu_ready, 1)

            def scan(q, i, r):
                c = q % NCH
                k = i * (2 * NPT) + (q * STEPS + 2 * r)
                for h in range(EH):
                    sl = (2 * r + h) % SLOTS
                    dve.wait_ge(dbu_ready, k + (h + 1))
                    dve.wait_ge(dA_ready, k + (h + 1))
                    if not (q == 0 and is0(i) and r < 2):
                        dve.wait_ge(prod_ready, k + (h + 1 - SLOTS))
                    initial = 0.0 if c == 0 else state[:, bass.ds(i * (2 * NPT) + (2 * r + h), 1)]
                    v_.tensor_tensor_scan(hs[:, sl, :], ps[:, DA + h, :], dbu[:, sl, :], initial, ALU.mult, ALU.add)\
                        .then_inc(h_ready, 1)

            def scan_state(q, i, r):
                if not (isinstance(i, int) and i * NPT + r == NST - 1):
                    drive(q, i + (r + 1) // NPT, (r + 1) % NPT)
                scan(q, i, r)

            def gate(q):
                b, c = q // NCH, q % NCH
                dve.wait_ge(y_added, STEPS * (q + 1))
                for h in range(EH):
                    v_.tensor_tensor(y2[:, h, :], ps[:, YY + h, :], zs[:, b, h, c * CH:(c + 1) * CH], ALU.mult).then_inc(y2_ready, 1)

            def add_mamba(q):
                b, c = q // NCH, q % NCH
                dve.wait_ge(side_copied, DONE["out", q])
                dve.wait_ge(x_added, b + 1)
                xs = flat(x_of(b)[:, TPC * c:TPC * (c + 1), :])
                chain.link(v_.tensor_tensor(xs, y2[:, 0, :], xs, ALU.add))

            def ffn(ffns):
                units = [(norm, v) for norm in ffns for v in range(8)]

                def arg(norm, v):
                    U = 8 * FFNS.index(norm) + v
                    sl, f = U % SLOTS, v % FC
                    dve.wait_ge(hid_ready, U + 1)
                    v_.tensor_scalar(tbuf[:, sl, :], hid[:, sl, :], 0.1, theta[:, f:f + 1], ALU.mult, ALU.add).then_inc(sum_ready, 1)

                def arg_less_theta(norm, v):
                    U = 8 * FFNS.index(norm) + v
                    sl, f = U % SLOTS, v % FC
                    dve.wait_ge(sum_ready, U + 1)
                    v_.tensor_scalar(tbuf[:, sl, :], tbuf[:, sl, :], theta[:, f:f + 1], None, ALU.subtract).then_inc(arg_ready, 1)

                def whole_turns(norm, v):
                    U = 8 * FFNS.index(norm) + v
                    sl = U % SLOTS
                    dve.wait_ge(turns_ready, U + 1)
                    v_.tensor_scalar(jbuf[:, sl, :], turn[:, sl, :], ROUND, ROUND, ALU.add, ALU.subtract).then_inc(whole_ready, 1)

                def quantum(norm, v):
                    U = 8 * FFNS.index(norm) + v
                    sl, f = U % SLOTS, v % FC
                    dve.wait_ge(sin_ready, U + 1)
                    if U >= SLOTS:
                        dve.wait_ge(act_used, U - SLOTS + 1)
                    v_.scalar_tensor_tensor(act_sb[:, sl, :], sn[:, sl, :], coef[:, f:f + 1], hid[:, sl, :], ALU.mult, ALU.add)\
                        .then_inc(q_ready, 1)

                def add_out(norm, t):
                    fi = FFNS.index(norm)
                    dve.wait_ge(act_used, fi * 8 + 4 * t + 4)
                    dve.wait_ge(x_added, ADDS.index(norm) + 1)
                    xs = flat(x_of(norm[1])[:, 4 * t:4 * t + 4, :])
                    v_.tensor_tensor(xs, ps[:, 7 if t == 0 else 0, :], xs, ALU.add).then_inc(out_read, 1)

                n_units = len(units)
                for n in range(n_units + 6):
                    if n < n_units:
                        arg(*units[n])
                    if n >= 1 and n - 1 < n_units:
                        whole_turns(*units[n - 1])
                    if n >= 2 and n - 2 < n_units:
                        quantum(*units[n - 2])
                    if n < n_units:
                        arg_less_theta(*units[n])
                    if n >= 5 and (n - 5) % 4 == 3:
                        add_out(units[n - 5][0], units[n - 5][1] // 4)
                        if units[n - 5][1] == 7 and units[n - 5][0][0] == "norm4":
                            dve.wait_ge(out_read, 2 * FFNS.index(units[n - 5][0]) + 2)
                            v_.engine_nop().then_inc(x_final, 1)
                dve.wait_ge(out_read, 2 * FFNS.index(ffns[-1]) + 2)

            def row_max(J, par, bank):
                dve.wait_ge(scores_ready, J + 1)
                v_.tensor_reduce(mx[:, par:par + 1], flat(ps[:, bank:bank + 2, :]), AX_X, ALU.max).then_inc(mx_ready, 1)
                dve.wait_ge(mx_ready, J + 1)
                v_.tensor_scalar(negm[:, par:par + 1], mx[:, par:par + 1], -QK, None, ALU.mult).then_inc(negm_ready, 1)

            def invert_sum(J, par, reuse):
                dve.wait_ge(probs_ready, J + 1)
                if reuse:
                    dve.wait_ge(attn_added, J - reuse + 1)
                v_.reciprocal(rinv[:, par:par + 1], rsum[:, par:par + 1]).then_inc(rinv_ready, 1)

            def add_attention(J, par, bank):
                dve.wait_ge(rinv_ready, J + 1)
                dve.wait_ge(attn_out, J + 1)
                xs = flat(x_tok[:, bass.ds(J, 1), :])
                v_.scalar_tensor_tensor(xs, ps[:, bank, 0:D], rinv[:, par:par + 1], xs, ALU.mult, ALU.add).then_inc(attn_added, 1)

            v_.memset(xin[:, :, 0:KCONV - 1], 0.0)
            dve.wait_ge(mamba_w_loaded, 16 * N_MAMBA)
            v_.tensor_scalar(win_sb[:, :], win_sb[:, :], normw_sb[:, :], None, ALU.mult).then_inc(win_scaled, 1)
            mamba_in(0, 0)
            dve.wait_ge(small_w_loaded, 16 * N_SMALL)
            kk, r = trig[:, 2, :], trig[:, 3, :]
            chain.link(v_.tensor_scalar(kk, theta[:, :], INV_2PI, ROUND, ALU.mult, ALU.add))
            chain.link(v_.tensor_scalar(kk, kk, ROUND, None, ALU.subtract))
            chain.link(v_.scalar_tensor_tensor(r, kk, -C1, theta[:, :], ALU.mult, ALU.add))
            chain.link(v_.scalar_tensor_tensor(r, kk, -C2, r, ALU.mult, ALU.add))
            chain.link(v_.scalar_tensor_tensor(rho[:, :], kk, -C3, r, ALU.mult, ALU.add))
            chain.link(v_.tensor_scalar(kk, rho[:, :], np.pi / 2, None, ALU.add))
            chain.link(v_.tensor_scalar(r, kk, np.pi, -TWO_PI, ALU.is_gt, ALU.mult))
            chain.link(v_.tensor_tensor(kk, kk, r, ALU.add))
            chain.add(v_.tensor_scalar(rho_turns[:, :], rho[:, :], INV_2PI, None, ALU.mult))
            chain.add(v_.tensor_scalar(trig[:, 0, :], rho[:, :], PI_LO, -PI_LO, ALU.min, ALU.max))
            v_.tensor_scalar(trig[:, 1, :], kk, PI_LO, -PI_LO, ALU.min, ALU.max).then_inc(trig_args, 1)
            dve.wait_ge(a_exp, 1)
            v_.tensor_scalar(a_sb[:, :, :], a_sb[:, :, :], -1.0, None, ALU.mult).then_inc(a_ready, 1)
            for p in range(1, 20):
                mamba_in(0, p)
            dve.wait_ge(consts_made, 2)
            for h in range(EH):
                v_.tensor_scalar(diag_d[:, h, :], ident[:, :], dpar_sb[:, h:h + 1], None, ALU.mult).then_inc(diag_ready, 1)
            dve.wait_ge(late_w_loaded, 16 * N_LATE)
            dve.wait_ge(trig_done, 1)
            chain.link(v_.tensor_tensor(trig[:, 6, :], trig[:, 5, :], wr_sb[:, :], ALU.mult))
            chain.link(v_.tensor_tensor(trig[:, 7, :], trig[:, 4, :], wi_sb[:, :], ALU.mult))
            chain.link(v_.tensor_tensor(trig[:, 6, :], trig[:, 6, :], trig[:, 7, :], ALU.add))
            chain.link(v_.tensor_tensor(trig[:, 6, :], trig[:, 6, :], wi_sb[:, :], ALU.mult))
            chain.link(v_.tensor_scalar(coef[:, :], trig[:, 6, :], 0.1, None, ALU.mult))
            for p in range(20, 37):
                mamba_in(0, p)
            for q in range(NCH):
                dve.wait_ge(du_ready, 1)
                drive(q, 0, 0)
                for n in range(NST):
                    scan_state(q, n // NPT, n % NPT)
                    mamba_in(1, NST * q + n)
                gate(q)
                if q == 1:
                    for p in range(32, 37):
                        mamba_in(1, p)
                add_mamba(q)
            layer_norm(FFNS[0])
            ffn(FFNS[0:1])
            layer_norm(("norm3", 0))
            for q in range(NCH, 2 * NCH):
                dve.wait_ge(du_ready, 2)
                drive(q, 0, 0)

                def tile(i, first, last):
                    J = i + (q - NCH) * NPT
                    for r in range(NPT):
                        if last:
                            scan_state(q, NST // NPT - 1, r)
                        else:
                            scan_state(q, i, r)
                        if r == 1:
                            row_max(J, 0, SIDE)
                        if r == 2 and not first:
                            add_attention(J - 1, 0, SIDE + 2)
                        if r == 3:
                            invert_sum(J, 0, 0 if first else 1)
                tile(0, q == NCH, False)
                with dve.Fori(1, NST // NPT - 1) as i:
                    tile(i, False, False)
                tile(NST // NPT - 1, False, True)
                gate(q)
                if q == 2 * NCH - 1:
                    add_attention(TILES - 1, 0, SIDE + 2)
                    dve.wait_ge(attn_added, TILES)
                    layer_norm(("norm4", 0))
                add_mamba(q)
            layer_norm(("norm2", 1))
            ffn(FFNS[1:3])
            layer_norm(("norm3", 1))

            def turned(J, par):
                dve.wait_ge(pT_in_psum, J * 2 + 2)
                dve.wait_ge(attn_out, J - 1)
                v_.tensor_copy(flat(pT[:, par, 4:8, :]), ps[:, 5, :]).then_inc(pT_high, 1)
                invert_sum(J, par, 2)

            for par in range(2):
                row_max(TILES + par, par, 2 * par)
            with dve.Fori(0, TILES // 2 - 1) as i:
                for par in range(2):
                    J = i * 2 + (TILES + par)
                    turned(J, par)
                    row_max(J + 2, par, 2 * par)
                    add_attention(J, par, 6 + par)
            for par in range(2):
                turned(2 * TILES - 2 + par, par)
                add_attention(2 * TILES - 2 + par, par, 6 + par)
            dve.wait_ge(attn_added, 2 * TILES)
            layer_norm(("norm4", 1))
            ffn(FFNS[3:4])

        @block.tensor
        def _(pe):
            mm = nc.tensor.matmul

            def side_bank(use, t):
                w = FIRST[use] + t
                if w >= 3:
                    pe.wait_ge(side_copied, w - 2)
                return SIDE + w % 3

            def turn_tokens(norm):
                for t in range(2):
                    pe.wait_ge(xn_ready, 2 * NORMS.index(norm) + t + 1)
                    bank = side_bank(norm, t)
                    for i in range(4):
                        ins = nc.tensor.transpose(ps[:, bank, i * P:(i + 1) * P], xn[:, 4 * t + i, :], ident[:, :])
                    ins.then_inc(side_filled, 1)

            def project(use, w, src):
                for t in range(2):
                    mm(ps[:, side_bank(use, t), :], w, src[:, t * CH:(t + 1) * CH], start=True, stop=True).then_inc(side_filled, 1)

            def project_u(use, w, rows):
                b = use[1]
                for t in range(2):
                    bank = side_bank(use, t)
                    for h in range(EH):
                        ins = mm(ps[0:rows, bank, :], w[:, h, :], u[:, b, h, t * CH:(t + 1) * CH], start=(h == 0), stop=(h == EH - 1))
                    ins.then_inc(side_filled, 1)

            def mamba_in(b, p):
                if p == 5:
                    turn_tokens(("norm1", b))
                elif p in (7, 9):
                    if p == 7:
                        pe.wait_ge(side_copied, DONE["norm1", b])
                    h = (p - 7) // 2
                    project((f"x{h}", b), win_v[:, 0, h, :], xnT[:, b, :])
                elif p in (11, 13):
                    h = (p - 11) // 2
                    project((f"z{h}", b), win_v[:, 1, h, :], xnT[:, b, :])
                elif p == 16:
                    pe.wait_ge(u_ready, b + 1)
                    project_u(("xdb", b), wx_sb, RANK + 2 * NST)
                elif p == 18:
                    if b == 0:
                        pe.wait_ge(wb3_ready, 1)
                    project_u(("b3", b), wb3_sb, B3)
                elif p in (20, 22):
                    h = (p - 20) // 2
                    pe.wait_ge(side_copied, DONE["xdb", b])
                    project((f"dt{h}", b), wdt_v[:, h, :], xdb[0:RANK, :])

            def b_row(q, i, r):
                b, c = q // NCH, q % NCH
                if not (q == 0 and is0(i) and r == 0):
                    pe.wait_ge(dbu_ready, i * (2 * NPT) + (q * STEPS + 2 * r))
                mm(ps[:, BB, :], flat(bsel[:, bass.ds(i * NPT + r, 1), :]), b3[:, b, c * CH:(c + 1) * CH],
                   start=True, stop=True).then_inc(B_ready, 1)

            def y_sum(q, i, r):
                for h in range(EH):
                    pe.wait_ge(prod_ready, i * (2 * NPT) + (q * STEPS + 2 * r + h + 1))
                    mm(ps[:, YY + h, :], ident[:, :], prod[:, (2 * r + h) % SLOTS, :], start=False, stop=True,
                       skip_group_check=True).then_inc(y_added, 1)

            def start_chunk(q):
                b, c = q // NCH, q % NCH
                b_row(q, 0, 0)
                b_row(q, 0, 1)
                if q:
                    pe.wait_ge(y2_ready, EH * q)
                for h in range(EH):
                    mm(ps[:, YY + h, :], diag_d[:, h, :], u[:, b, h, c * CH:(c + 1) * CH], start=True, stop=True)

            def scan_state(q, i, r):
                if not (isinstance(i, int) and i * NPT + r >= NST - 2):
                    b_row(q, i + (r + 2) // NPT, (r + 2) % NPT)
                if not (is0(i) and r == 0):
                    y_sum(q, i - (1 if r == 0 else 0), (r - 1) % NPT)

            def end_chunk(q):
                y_sum(q, NST // NPT - 1, NPT - 1)
                pe.wait_ge(y2_ready, EH * (q + 1))
                if q >= NCH:
                    pe.wait_ge(pT_high, (q - NCH + 1) * NPT)
                    pe.wait_ge(attn_added, (q - NCH + 1) * NPT - (1 if q < 2 * NCH - 1 else 0))
                bank = side_bank(("out", q), 0)
                for i in range(TPC):
                    for h in range(EH):
                        ins = mm(ps[:, bank, i * D:(i + 1) * D], y2[:, h, i * P:(i + 1) * P], wout_sb[:, h, :],
                                 start=(h == 0), stop=(h == EH - 1), skip_group_check=True)
                ins.then_inc(side_filled, 1)

            def ffn(ffns):
                units = [(norm, v) for norm in ffns for v in range(8)]

                def up(norm, v):
                    U = 8 * FFNS.index(norm) + v
                    f, t = v % FC, v // FC
                    if U >= 2:
                        pe.wait_ge(hid_ready, U - 1)
                    mm(ps[:, 5 + v % 2, :], w1_v[:, f, :], xnT[:, norm[1], t * CH:(t + 1) * CH], start=True, stop=True)\
                        .then_inc(hid_in_psum, 1)

                def down(norm, v):
                    fi = FFNS.index(norm)
                    U = 8 * fi + v
                    f, t = v % FC, v // FC
                    pe.wait_ge(act_ready, U + 1)
                    if f == 0 and fi:
                        pe.wait_ge(out_read, 2 * fi + t - 1)
                    for i in range(TPC):
                        ins = mm(ps[:, 7 if t == 0 else 0, i * D:(i + 1) * D], act_sb[:, U % SLOTS, i * P:(i + 1) * P], w2_sb[:, f, :],
                                 start=(f == 0 and i == 0), stop=(f == FC - 1), skip_group_check=True)
                    ins.then_inc(act_used, 1)

                pe.wait_ge(side_copied, DONE[ffns[-1]])
                up(*units[0])
                up(*units[1])
                for n in range(len(units) + 4):
                    if n >= 4:
                        down(*units[n - 4])
                    if n + 2 < len(units):
                        up(*units[n + 2])

            def qkv(b):
                pe.wait_ge(side_copied, DONE["norm3", b])
                for j, w in enumerate((wq_sb, wk_sb)):
                    for t in range(2):
                        mm(ps[:, side_bank(("qkv", b), 2 * j + t), :], w[:, :], xnT[:, b, t * CH:(t + 1) * CH],
                           start=True, stop=True).then_inc(side_filled, 1)
                for t in range(2):
                    bank = side_bank(("qkv", b), 4 + t)
                    for i in range(4):
                        ins = mm(ps[:, bank, i * D:(i + 1) * D], xnT[:, b, (4 * t + i) * P:(4 * t + i + 1) * P], wv_sb[:, :],
                                 start=True, stop=True, skip_group_check=True)
                    ins.then_inc(side_filled, 1)

            def scores(kt, b, bank):
                for t in range(2):
                    ins = mm(ps[:, bank + t, :], kt, qT(b)[:, t * CH:(t + 1) * CH], start=True, stop=True)
                ins.then_inc(scores_ready, 1)

            def turn_probs(J, par, banks, reuse):
                pe.wait_ge(probs_ready, J + 1)
                for t in range(2):
                    if reuse:
                        pe.wait_ge(pT_low if t == 0 else pT_high, J)
                    for i in range(4):
                        ins = nc.tensor.transpose(ps[:, banks + t, i * P:(i + 1) * P], pm[:, par, (4 * t + i) * P:(4 * t + i + 1) * P], ident[:, :])
                    ins.then_inc(pT_in_psum, 1)

            def p_v(J, par, bank, reuse):
                pe.wait_ge(pT_low, J + 1)
                pe.wait_ge(pT_high, J + 1)
                if reuse == 1:
                    pe.wait_ge(rinv_ready, J + 1)
                elif reuse:
                    pe.wait_ge(attn_added, J - reuse + 1)
                for i in range(TILES):
                    ins = mm(ps[:, bank, 0:D], pT[:, par, i, :], vt[:, i, :], start=(i == 0), stop=(i == TILES - 1))
                ins.then_inc(attn_out, 1)

            pe.wait_ge(consts_made, 2)
            pe.wait_ge(mamba_w_loaded, 16 * N_MAMBA)
            pe.wait_ge(win_scaled, 1)
            for p in range(24):
                mamba_in(0, p)
            pe.wait_ge(consts_made, 3)
            pe.wait_ge(b3_ready, 1)
            pe.wait_ge(diag_ready, EH)
            for q in range(NCH):
                start_chunk(q)
                for n in range(NST):
                    scan_state(q, n // NPT, n % NPT)
                    mamba_in(1, NST * q + n)
                end_chunk(q)
            pe.wait_ge(late_w_loaded, 16 * N_LATE)
            turn_tokens(FFNS[0])
            ffn(FFNS[0:1])
            turn_tokens(("norm3", 0))
            qkv(0)
            pe.wait_ge(side_copied, DONE["qkv", 0])
            pe.wait_ge(b3_ready, 2)
            for q in range(NCH, 2 * NCH):
                start_chunk(q)

                def tile(i, first, last):
                    J = i + (q - NCH) * NPT
                    for r in range(NPT):
                        if r == 1 and not first:
                            p_v(J - 1, 0, SIDE + 2, 1)
                        scan_state(q, i, r)
                        if r == 0:
                            pe.wait_ge(kstat_ready, J + 1)
                            if not first:
                                pe.wait_ge(pT_high, J)
                            if q > NCH and is0(i):
                                pe.wait_ge(side_copied, DONE["out", q - 1])
                            scores(kstat[:, :], 0, SIDE)
                        if r == 2:
                            turn_probs(J, 0, SIDE, 0)
                tile(0, q == NCH, False)
                with pe.Fori(1, NST // NPT - 1) as i:
                    tile(i, False, False)
                tile(NST // NPT - 1, False, True)
                if q == 2 * NCH - 1:
                    p_v(TILES - 1, 0, SIDE + 2, 1)
                end_chunk(q)
            turn_tokens(("norm4", 0))
            turn_tokens(("norm2", 1))
            ffn(FFNS[1:3])
            turn_tokens(("norm3", 1))
            qkv(1)
            pe.wait_ge(side_copied, DONE["qkv", 1])

            def scores1(j):
                if j >= 2:
                    pe.wait_ge(probs_ready, TILES + j - 1)
                scores(kT(1)[:, j * P:(j + 1) * P], 1, 2 * (j % 2))

            scores1(0)
            scores1(1)
            for j in range(TILES):
                turn_probs(TILES + j, j % 2, 4, True)
                if j + 2 < TILES:
                    scores1(j + 2)
                p_v(TILES + j, j % 2, 6 + j % 2, 2)
            turn_tokens(("norm4", 1))
            ffn(FFNS[3:4])


_INS = ['L0_attn_a_hidden_states', 'L0_attn_a_norm_w', 'L0_attn_a_W_in', 'L0_attn_a_conv_w', 'L0_attn_a_W_x',
        'L0_attn_a_W_dt', 'L0_attn_a_b_dt', 'L0_attn_a_A_log', 'L0_attn_a_D_param', 'L0_attn_a_W_out',
        'L0_attn_b_W_query', 'L0_attn_b_W_key', 'L0_attn_b_W_value', 'L0_ffn_W1', 'L0_ffn_b1',
        'L0_ffn_quantum_phases', 'L0_ffn_quantum_weights_real', 'L0_ffn_quantum_weights_imag', 'L0_ffn_W2', 'L0_ffn_b2']
_OUTS = [((BATCH, SEQ, D), 'float32')]


def kernel(**inputs):
    import concourse.bacc as _bacc
    from concourse.bass_utils import run_bass_kernel_spmd as _run

    nc = _bacc.Bacc("TRN2", target_bir_lowering=False, num_devices=1)
    arrays, args = {}, []
    for name in _INS:
        a = np.ascontiguousarray(inputs[name])
        arrays[f"in_{name}_dram"] = a
        args.append(nc.dram_tensor(f"in_{name}_dram", a.shape, mybir.dt.from_np(a.dtype), kind="ExternalInput").ap())
    for i, (shape, dtype) in enumerate(_OUTS):
        args.append(nc.dram_tensor(f"out_{i}_dram", shape, mybir.dt.from_np(np.dtype(dtype)), kind="ExternalOutput").ap())
    build(nc, *args)
    r = _run(nc, [arrays], core_ids=[0])
    return tuple(r.results[0][f"out_{i}_dram"] for i in range(len(_OUTS)))[0]
```

```python
from contextlib import ExitStack

import numpy as np

import concourse.bass as bass
from concourse import mybir

ALU = mybir.AluOpType
ACT = mybir.ActivationFunctionType
AX_X = mybir.AxisListType.X
F32 = mybir.dt.float32
BF16 = mybir.dt.bfloat16

P = 128
BATCH, SEQ, D = 2, 1024, 128
TILES = SEQ // P
E, NST, RANK, KCONV = 256, 16, 64, 4
EH = E // P
F = 512
FC = F // P
CH = 512
NCH = SEQ // CH
TPC = CH // P
B3 = 96
SLOTS = 4
STEPS = NST * EH
NPT = 4
QK = float(1.0 / np.sqrt(D))
LN_EPS, RMS_EPS = 1e-5, 1e-6

ROUND = 1.5 * 2.0 ** 23
TWO_PI = 2.0 * np.pi
INV_2PI = float(np.float32(1.0 / TWO_PI))
C1 = 6.28125
C2 = float(np.round((TWO_PI - C1) * 2.0 ** 20) / 2.0 ** 20)
C3 = float(TWO_PI - C1 - C2)
PI_LO = float(np.nextafter(np.float32(np.pi), np.float32(0)))
ATANH = (2.0000000076817575, 0.6666632164139702, 0.4002459522991947, 0.27965157756134756, 0.28157778314218707)

I32 = mybir.dt.int32
ROOT_GUESS = 0x5f3759df

DA, BB, YY, SIDE = 0, 2, 3, 5
UP, SUM = 1, (0, 3)
TAIL = 13


def outs(name, k):
    return [(name + "_out", k, h) for h in range(EH)]


def convolved(k, h):
    return [("x", k, h, 0), ("x", k, h, 1)]


NORM_FIRST = [("norm", 0, p) for p in range(5)]
TURN_FIRST = [("turn", 0), ("turn", 1), ("turned", 0), ("turned", 1), ("norm", 0, 5)]
ALONE = (
    convolved(0, 0) + [("norm", 1, 0), ("x_out", 0, 0)] + convolved(0, 1) + [("x_out", 0, 1), ("z", 0, 0), ("z", 0, 1)] + outs("z", 0)
    + [("exp_tables", 0), ("norm", 1, 1), ("xdb", 0), ("xdb_out", 0), ("dt", 0, 0), ("dt", 0, 1), ("norm", 1, 2)] + outs("dt", 0)
    + [("norm", 1, 3), ("b3", 0), ("tail", 0, 0), ("norm", 1, 4), ("tail", 0, 1), ("b3_out", 0), ("b3_high", 0), ("b3_rest", 0), ("norm", 1, 5)]
    + [("tail", 0, 2), ("tail", 0, 3), ("turn", 2), ("turn", 3), ("tail", 0, 4), ("b3_mid", 0), ("turned", 2), ("turned", 3)]
    + [("tail", 0, 5), ("b3_low", 0), ("tail", 0, 6), ("silu_tables", 1)] + convolved(1, 0) + [("x_out", 1, 0)] + convolved(1, 1)
    + [("x_out", 1, 1), ("z", 1, 0), ("z", 1, 1)] + outs("z", 1) + [("exp_tables", 1)] + [("tail", 0, p) for p in range(7, TAIL)]
)
BESIDE = [
    [("xdb", 1)],
    [("xdb_out", 1), ("dt", 1, 0), ("dt", 1, 1)],
    outs("dt", 1) + [("b3", 1), ("tail", 1, 0)],
    [("b3_out", 1), ("x", 2, 0, 0), ("tail", 1, 1)],
    [("b3_high", 1), ("x", 2, 0, 1), ("tail", 1, 2)],
    [("x_out", 2, 0), ("x", 2, 1, 0), ("b3_rest", 1), ("tail", 1, 3)],
    [("x", 2, 1, 1), ("b3_mid", 1), ("tail", 1, 4)],
    [("x_out", 2, 1), ("x", 3, 0, 0), ("b3_low", 1), ("tail", 1, 5)],
    [("x", 3, 0, 1), ("tail", 1, 6)],
    [("x_out", 3, 0), ("x", 3, 1, 0), ("tail", 1, 7)],
    [("x", 3, 1, 1), ("tail", 1, 8)],
    [("x_out", 3, 1), ("silu", 2), ("z", 2, 0), ("z", 2, 1), ("tail", 1, 9), ("tail", 1, 10)],
    outs("z", 2) + [("z", 3, 0), ("z", 3, 1), ("tail", 1, 11), ("tail", 1, 12)],
    outs("z", 3) + [("xdb", 2)],
    [("xdb_out", 2), ("xdb", 3)],
    [("xdb_out", 3)],
    [("dt", 2, 0), ("dt", 2, 1)],
    outs("dt", 2) + [("tail", 2, 0)],
    [("dt", 3, 0), ("dt", 3, 1), ("tail", 2, 1)],
    outs("dt", 3) + [("tail", 2, 2)],
    [("b3", 2), ("tail", 2, 3), ("tail", 3, 0)],
    [("b3_out", 2), ("tail", 2, 4), ("tail", 3, 1)],
    [("b3_high", 2), ("b3", 3), ("tail", 2, 5), ("tail", 3, 2)],
    [("b3_out", 3), ("b3_rest", 2), ("tail", 2, 6), ("tail", 3, 3)],
    [("b3_mid", 2), ("b3_high", 3), ("tail", 2, 7), ("tail", 3, 4)],
    [("b3_low", 2), ("tail", 2, 8), ("tail", 3, 5)],
    [("b3_rest", 3), ("tail", 2, 9), ("tail", 3, 6)],
    [("b3_mid", 3), ("tail", 2, 10), ("tail", 3, 7)],
    [("b3_low", 3), ("tail", 2, 11), ("tail", 3, 8)],
    [("half_turn", 0), ("tail", 2, 12), ("tail", 3, 9)],
    [("half_turned", 0), ("tail", 3, 10), ("tail", 3, 11)],
    [("tail", 3, 12)],
]


HALVES = [("norm2", 0, 0), ("norm2", 0, 1), ("norm3", 0, 0), ("norm3", 0, 1), ("norm4", 0, 0), ("norm2", 1, 0),
          ("norm4", 0, 1), ("norm2", 1, 1), ("norm3", 1, 0), ("norm3", 1, 1), ("norm4", 1, 0), ("norm4", 1, 1)]
GROUPS = [h for h in HALVES if h[0] != "norm3"]
HT = TILES // 2


NORM_PARTS = 15
for _p in range(NORM_PARTS):
    BESIDE[25 + _p // 4].append(("half_norm", 0, _p))


def side_use(step):
    name, k = step[:2]
    if name == "half_turn":
        return [("half", k, 1)]
    if name in ("turn", "xdb", "b3"):
        return [(name, k, 1)]
    if name in ("z", "dt") or name == "x" and step[3] == 0:
        return [(f"{name}{step[2]}", k, 1)]
    return []


SIDE_USES = (
    sum((side_use(s) for s in TURN_FIRST + ALONE), [])
    + sum((side_use(s) for n in range(NST + 6) for s in BESIDE[n]), []) + [("out", 0, 1)]
    + sum((side_use(s) for n in range(NST + 6, 2 * NST) for s in BESIDE[n]), []) + [("out", 1, 1)]
    + [("half", 1, 1), ("half", 2, 1), ("qkv", (0, 0), 3), ("half", 3, 1), ("qkv", (0, 1), 3), ("out", 2, 1),
       ("half", 4, 1), ("half", 5, 1), ("out", 3, 1), ("half", 6, 1), ("half", 7, 1),
       ("half", 8, 1), ("qkv", (1, 0), 3), ("half", 9, 1), ("qkv", (1, 1), 3), ("half", 10, 1), ("half", 11, 1)]
)
FIRST, DONE = {}, {}
BANK, BEFORE = [], []
for _s, _b, _n in SIDE_USES:
    FIRST[_s, _b] = len(BANK)
    for _i in range(_n):
        _bank = SIDE + 2 if (_s, _b) == ("out", 2) else SIDE + (BANK[-1] - SIDE + 1) % 3 if BANK else SIDE
        BEFORE.append(len(BANK) - BANK[::-1].index(_bank) if _bank in BANK else 0)
        BANK.append(_bank)
    DONE[_s, _b] = len(BANK)


def build(nc, hidden, norm_w, w_in, conv_w, w_x, w_dt, b_dt, a_log, d_param, w_out,
          w_q, w_k, w_v, w1, b1, phases, q_real, q_imag, w2, b2, out):
    with ExitStack() as ctx:
        def sb(name, shape, dt=F32):
            return ctx.enter_context(nc.sbuf_tensor(name, shape, dt))

        def sem(name):
            return ctx.enter_context(nc.semaphore(name))

        x_tok = sb("x_tok", [P, BATCH * TILES, D])
        xn = sb("xn", [P, TILES, D])
        xnT = sb("xnT", [P, BATCH, KCONV - 1 + SEQ])
        win_sb = sb("win_sb", [P, 2 * E])
        wx_sb = sb("wx_sb", [P, EH, RANK + 2 * NST])
        wdt_sb = sb("wdt_sb", [RANK, E])
        wout_sb = sb("wout_sb", [P, EH, D])
        w1_sb = sb("w1_sb", [P, F])
        w2_sb = sb("w2_sb", [P, FC, D])
        wq_sb = sb("wq_sb", [P, D])
        wk_sb = sb("wk_sb", [P, D])
        wv_sb = sb("wv_sb", [P, D])
        normw_sb = sb("normw_sb", [P, 1])
        convw_sb = sb("convw_sb", [P, E * KCONV])
        wconv = sb("wconv", [P, KCONV, E])
        bdt_sb = sb("bdt_sb", [P, EH])
        dpar_sb = sb("dpar_sb", [P, EH])
        a_sb = sb("a_sb", [P, EH, NST])
        b1_sb = sb("b1_sb", [P, FC])
        theta = sb("theta", [P, FC])
        wr_sb = sb("wr_sb", [P, FC])
        wi_sb = sb("wi_sb", [P, FC])
        b2_sb = sb("b2_sb", [P, D])
        rho = sb("rho", [P, FC])
        rho_turns = sb("rho_turns", [P, FC])
        trig = sb("trig", [P, 8, FC])
        coef = sb("coef", [P, FC])
        ident = sb("ident", [P, P])
        diag_d = sb("diag_d", [P, EH, P])
        bsel = sb("bsel", [B3, NST, P], BF16)
        wb3_sb = sb("wb3_sb", [P, EH, B3])
        b3 = sb("b3", [B3, BATCH, SEQ], BF16)
        b3_mid = sb("b3_mid", [B3, CH], BF16)
        b3_rest = sb("b3_rest", [B3, CH])
        two = sb("two", [P, 1])

        stats = sb("stats", [P, TILES, 6])
        mv = sb("mv", [P, TILES, 2])
        var_eps = sb("var_eps", [P, TILES])
        rstd0 = sb("rstd0", [P, TILES])
        newton = sb("newton", [P, TILES])
        rstd = sb("rstd", [P, TILES])
        rstd2 = sb("rstd2", [P, TILES])

        u = sb("u", [P, BATCH, EH, SEQ])
        zs = sb("zs", [P, BATCH, EH, SEQ])
        delta = sb("delta", [P, BATCH, EH, SEQ])
        du = sb("du", [P, BATCH, EH, SEQ])
        xdb = sb("xdb", [RANK + 2 * NST, SEQ])
        ebuf = sb("ebuf", [P, EH, SEQ])
        sbuf_ = sb("sbuf_", [P, EH, SEQ])
        s2buf = sb("s2buf", [P, EH, SEQ])
        c_all = sb("c_all", [P, NST, CH])
        dbu = sb("dbu", [P, SLOTS, CH])
        hs = sb("hs", [P, SLOTS, CH])
        prod = sb("prod", [P, SLOTS, CH])
        state = sb("state", [P, STEPS])
        y2 = sb("y2", [P, EH, CH])
        kstat = sb("kstat", [P, P])
        rsum = sb("rsum", [P, 2])
        mx = sb("mx", [P, 2])
        negm = sb("negm", [P, 2])
        rinv = sb("rinv", [P, 2])

        def as_slots(t):
            return t.rearrange("p h (s t) -> p (h s) t", t=CH)

        x1 = convw_sb[:, :].rearrange("p (i d) -> p i d", d=D)
        hid, tbuf, turn = as_slots(ebuf[:, :, :]), as_slots(sbuf_[:, :, :]), as_slots(s2buf[:, :, :])
        jbuf, sn, act_sb = as_slots(zs[:, 0, :, :]), as_slots(delta[:, 0, :, :]), as_slots(u[:, 0, :, :])
        pm = jbuf[:, :, :].rearrange("p (a s) t -> p a (s t)", a=2)
        pT = sn[:, :, :].rearrange("p (a s) (i d) -> p a (s i) d", a=2, d=P)
        vt = ebuf[:, 0, :].rearrange("p (i d) -> p i d", d=D)

        def qT(b):
            return du[:, b, 0, :]

        def kT(b):
            return du[:, b, 1, :]

        c_dram = nc.dram_tensor("c_scratch", [BATCH, NST, SEQ], F32, kind="Internal").ap()
        ps = ctx.enter_context(nc.psum_tensor("ps", [P, 8, CH], F32))

        x_loaded = [sem(f"x_loaded{b}") for b in range(BATCH)]
        mamba_w_loaded = sem("mamba_w_loaded")
        small_w_loaded = sem("small_w_loaded")
        late_w_loaded = sem("late_w_loaded")
        consts_made = sem("consts_made")
        wb3_ready = sem("wb3_ready")
        pool_chain = sem("pool_chain")
        act_chain = sem("act_chain")
        dve_chain = sem("dve_chain")
        win_scaled = sem("win_scaled")
        diag_ready = sem("diag_ready")
        trig_args = sem("trig_args")
        trig_done = sem("trig_done")
        a_exp = sem("a_exp")
        a_ready = sem("a_ready")
        side_filled = sem("side_filled")
        side_copied = sem("side_copied")
        xn_ready = sem("xn_ready")
        x1_ready = sem("x1_ready")
        x_added = sem("x_added")
        wconv_ready = sem("wconv_ready")
        u_ready = sem("u_ready")
        z_ready = sem("z_ready")
        b3_high = sem("b3_high")
        b3_rest_ready = sem("b3_rest_ready")
        b3_mid_ready = sem("b3_mid_ready")
        b3_ready = sem("b3_ready")
        relu_part = sem("relu_part")
        e_ready = sem("e_ready")
        s_ready = sem("s_ready")
        s2_ready = sem("s2_ready")
        delta_ready = sem("delta_ready")
        du_ready = sem("du_ready")
        c_stored = sem("c_stored")
        c_loaded = sem("c_loaded")
        dA_ready = sem("dA_ready")
        B_ready = sem("B_ready")
        dbu_ready = sem("dbu_ready")
        h_ready = sem("h_ready")
        prod_ready = sem("prod_ready")
        y_added = sem("y_added")
        y2_ready = sem("y2_ready")
        hid_in_psum = sem("hid_in_psum")
        hid_ready = sem("hid_ready")
        sum_ready = sem("sum_ready")
        part_ready = sem("part_ready")
        turns_ready = sem("turns_ready")
        arg_ready = sem("arg_ready")
        whole_ready = sem("whole_ready")
        sin_ready = sem("sin_ready")
        q_ready = sem("q_ready")
        act_ready = sem("act_ready")
        act_used = sem("act_used")
        out_read = sem("out_read")
        kstat_ready = sem("kstat_ready")
        scores_ready = sem("scores_ready")
        mx_ready = sem("mx_ready")
        negm_ready = sem("negm_ready")
        probs_ready = sem("probs_ready")
        rinv_ready = sem("rinv_ready")
        pT_in_psum = sem("pT_in_psum")
        pT_low = sem("pT_low")
        pT_high = sem("pT_high")
        attn_out = sem("attn_out")
        attn_added = sem("attn_added")
        x_final = sem("x_final")
        stored = sem("stored")

        class Chain:
            def __init__(self, eng, s):
                self.eng, self.s, self.n = eng, s, 0

            def add(self, ins):
                ins.then_inc(self.s, 1)
                self.n += 1

            def wait(self):
                self.eng.wait_ge(self.s, self.n)

            def link(self, ins):
                self.add(ins)
                self.wait()

        def is0(v):
            return isinstance(v, int) and v == 0

        x_dram = hidden.rearrange("b (t p) d -> b p t d", p=P)
        out_dram = out.rearrange("b (t p) d -> b p t d", p=P)

        def x_of(b):
            return x_tok[:, b * TILES:(b + 1) * TILES, :]

        def half_of(b, h):
            return x_of(b)[:, h * HT:(h + 1) * HT, :]

        def flat(ap):
            return ap.rearrange("p a t -> p (a t)")

        def cols(k):
            return slice(k % NCH * CH, (k % NCH + 1) * CH)

        def b3_full(k):
            return du[0:B3, k // NCH, 0, cols(k)]

        def xT_of(b):
            return xnT[:, b, KCONV - 1:]

        win_v = win_sb[:, :].rearrange("k (s p c) -> k s c p", s=2, c=EH)
        wconv_v = wconv[:, :, :].rearrange("k j (p c) -> k j c p", c=EH)
        wdt_v = wdt_sb[:, :].rearrange("k (p c) -> k c p", c=EH)
        w1_v = w1_sb[:, :].rearrange("k (p c) -> k c p", c=FC)
        N_SMALL, N_MAMBA, N_LATE = 5, 5, 9

        block = ctx.enter_context(nc.Block())

        @block.sync
        def _(sp):
            sp.dma_start(x_of(0), x_dram[0]).then_inc(x_loaded[0], 16)
            sp.dma_start(win_sb[:, :], w_in).then_inc(mamba_w_loaded, 16)
            sp.dma_start(normw_sb[:, :], norm_w.rearrange("(p o) -> p o", o=1)).then_inc(mamba_w_loaded, 16)
            sp.dma_start(wx_sb[:, :, :], w_x.rearrange("(p c) r -> p c r", c=EH)).then_inc(mamba_w_loaded, 16)
            sp.dma_start(wdt_sb[:, :], w_dt).then_inc(mamba_w_loaded, 16)
            sp.dma_start(wout_sb[:, :, :], w_out.rearrange("(p c) d -> p c d", c=EH)).then_inc(mamba_w_loaded, 16)
            sp.dma_start(convw_sb[:, :], conv_w.rearrange("e o k -> (e o k)").partition_broadcast(P)).then_inc(small_w_loaded, 16)
            sp.dma_start(a_sb[:, :, :], a_log.rearrange("(p c) n -> p c n", c=EH)).then_inc(small_w_loaded, 16)
            sp.dma_start(bdt_sb[:, :], b_dt.rearrange("(p c) -> p c", c=EH)).then_inc(small_w_loaded, 16)
            sp.dma_start(dpar_sb[:, :], d_param.rearrange("(p c) -> p c", c=EH)).then_inc(small_w_loaded, 16)
            sp.dma_start(theta[:, :], phases.rearrange("(p c) -> p c", c=FC)).then_inc(small_w_loaded, 16)
            sp.dma_start(x_of(1), x_dram[1]).then_inc(x_loaded[1], 16)
            for dst, src in ((b1_sb, b1), (wr_sb, q_real), (wi_sb, q_imag)):
                sp.dma_start(dst[:, :], src.rearrange("(p c) -> p c", c=FC)).then_inc(late_w_loaded, 16)
            sp.dma_start(b2_sb[:, :], b2.partition_broadcast(P)).then_inc(late_w_loaded, 16)
            sp.dma_start(w1_sb[:, :], w1).then_inc(late_w_loaded, 16)
            sp.dma_start(w2_sb[:, :, :], w2.rearrange("(p c) d -> p c d", c=FC)).then_inc(late_w_loaded, 16)
            for dst, src in ((wq_sb, w_q), (wk_sb, w_k), (wv_sb, w_v)):
                sp.dma_start(dst[:, :], src).then_inc(late_w_loaded, 16)

            for q in range(BATCH * NCH):
                b, c = q // NCH, q % NCH
                sp.wait_ge(side_copied, DONE["xdb", q])
                sp.dma_start(c_dram[b, :, c * CH:(c + 1) * CH], xdb[RANK + NST:RANK + 2 * NST, cols(q)]).then_inc(c_stored, 16)
                sp.wait_ge(c_stored, 16 * (q + 1))
                for g in range(NST // 2):
                    if q:
                        sp.wait_ge(prod_ready, STEPS * (q - 1) + 4 * (g + 1))
                    src = c_dram[b, 2 * g:2 * g + 2, c * CH:(c + 1) * CH].partition_broadcast(P)
                    sp.dma_start(c_all[:, 2 * g:2 * g + 2, :], src).then_inc(c_loaded, 16)
                    sp.wait_ge(c_loaded, 16 * (q * NST // 2 + g + 1))
            finals = [g for g in GROUPS if g[0] == "norm4"]
            for i, (_, b, h) in enumerate(finals):
                sp.wait_ge(x_final, i + 1)
                sp.dma_start(out_dram[b][:, h * HT:(h + 1) * HT, :], half_of(b, h)).then_inc(stored, 16)
            sp.wait_ge(stored, 16 * len(finals))

        @block.gpsimd
        def _(pool):
            chain = Chain(pool, pool_chain)
            g = nc.gpsimd
            g.memset(two[:, :], 2.0).then_inc(consts_made, 1)
            chain.link(g.memset(ident[:, :], 0.0))
            g.affine_select(out=ident[:, :], in_=ident[:, :], compare_op=ALU.not_equal, fill=1.0, base=0,
                            pattern=[[-1, P]], channel_multiplier=1).then_inc(consts_made, 1)
            chain.link(g.memset(wb3_sb[:, :, :], 0.0))
            pool.wait_ge(mamba_w_loaded, 16 * N_MAMBA)
            for part in range(3):
                ins = g.tensor_copy(wb3_sb[:, :, 32 * part:32 * part + NST], wx_sb[:, :, RANK:RANK + NST])
            ins.then_inc(wb3_ready, 1)
            chain.link(g.memset(bsel[:, :, :], 0.0))
            for part in range(3):
                ins = g.affine_select(out=bsel[:, :, :], in_=bsel[:, :, :], compare_op=ALU.not_equal, fill=1.0,
                                      base=-32 * part, pattern=[[-1, NST], [0, P]], channel_multiplier=1)
                if part < 2:
                    chain.link(ins)
            ins.then_inc(consts_made, 1)

            def products(q, i, r):
                k = i * (2 * NPT) + (q * STEPS + 2 * r)
                c_row = flat(c_all[:, bass.ds(i * NPT + r, 1), :])
                for h in range(EH):
                    if h == 0 and r % 2 == 0:
                        pool.wait_ge(c_loaded, i * 32 + (16 * (q * NST // 2 + r // 2 + 1)))
                    pool.wait_ge(h_ready, k + (h + 1))
                    if not (q == 0 and is0(i) and r < 2):
                        pool.wait_ge(y_added, k + (h + 1 - SLOTS))
                    if not isinstance(i, int):
                        pool.nop(nofuse=True)
                    sl = (2 * r + h) % SLOTS
                    g.tensor_tensor(prod[:, sl, :], hs[:, sl, :], c_row, ALU.mult).then_inc(prod_ready, 1)

            def key_tile(J, col, first):
                if not first:
                    pool.wait_ge(scores_ready, J)
                if not isinstance(J, int):
                    pool.nop(nofuse=True)
                g.tensor_copy(kstat[:, :], kT(0)[:, bass.ds(col, P)]).then_inc(kstat_ready, 1)

            def ffn(groups):
                for g_ in groups:
                    i = HALVES.index(GROUPS[g_])
                    xh = half_of(*GROUPS[g_][1:])
                    pool.wait_ge(xn_ready, 2 * BATCH + i + 1)
                    g.tensor_tensor(xh, xh, b2_sb[:, :].unsqueeze(1).to_broadcast([P, HT, D]), ALU.add).then_inc(x_added, 1)
                    for f in range(FC):
                        U = FC * g_ + f
                        sl = U % SLOTS
                        pool.wait_ge(whole_ready, U + 1)
                        g.tensor_tensor(jbuf[:, sl, :], turn[:, sl, :], jbuf[:, sl, :], ALU.subtract).then_inc(part_ready, 1)

            def step(name, k, *args):
                if name == "tail" and k >= NCH and args[0] == 12:
                    b = k // NCH
                    pool.wait_ge(delta_ready, k - NCH + 1)
                    g.tensor_tensor(du[:, b, :, cols(k)], delta[:, b, :, cols(k)], u[:, b, :, cols(k)], ALU.mult).then_inc(du_ready, 1)

            def beside(n):
                for st in BESIDE[n]:
                    step(*st)

            def add_ln(b):
                pool.wait_ge(x1_ready, b + 1)
                pool.wait_ge(xn_ready, 2 * b + 2)
                g.tensor_tensor(x_of(b), x_of(b), x1, ALU.add).then_inc(x_added, 1)

            add_ln(0)
            add_ln(1)
            for q in range(NCH):
                for n in range(NST):
                    products(q, n // NPT, n % NPT)
                    beside(NST * q + n)
            ffn((0, 1))
            pool.wait_ge(side_copied, DONE["qkv", (0, 1)])
            key_tile(0, 0, True)
            for q in range(NCH, 2 * NCH):
                def tile(i, first):
                    J = i + (q - NCH) * NPT
                    for r in range(NPT):
                        products(q, i, r)
                        if r == 1 and not (q == 2 * NCH - 1 and first == "last"):
                            key_tile(J + 1, i * P + ((q - NCH) * NPT * P + P), False)
                tile(0, "first")
                with pool.Fori(1, NST // NPT - 1) as i:
                    tile(i, "")
                tile(NST // NPT - 1, "last")
            ffn((2, 3, 4, 5))
            ffn((6, 7))

        @block.scalar
        def _(act):
            chain = Chain(act, act_chain)
            s = nc.scalar

            def exp_tables():
                s.preload_act_table_set("natural_log_exp_and_others")

            def silu_sin_tables():
                s.preload_act_table_set("silu_and_others")

            def copy_out(use, dsts, rows=P, bias=None, func=None):
                for t, dst in enumerate(dsts):
                    w = FIRST[use] + t
                    act.wait_ge(side_filled, w + 1)
                    src = ps[0:rows, BANK[w], :]
                    if func is not None:
                        s.activation(dst, src, func).then_inc(side_copied, 1)
                    elif bias is None:
                        s.copy(dst, src).then_inc(side_copied, 1)
                    else:
                        s.activation(dst, src, ACT.Identity, bias=bias).then_inc(side_copied, 1)

            def halves(ap):
                return [ap[:, t * CH:(t + 1) * CH] for t in range(2)]

            def half_turned(i):
                _, b, h = HALVES[i]
                copy_out(("half", i), [xT_of(b)[:, cols(h)]])

            def step(name, k, *args):
                b = k // NCH
                if name == "turned":
                    copy_out(("turn", k), [xT_of(b)[:, cols(k)]])
                elif name == "half_turned":
                    half_turned(k)
                elif name in ("x_out", "z_out"):
                    h = args[0]
                    copy_out((f"{name[0]}{h}", k), [(u if name == "x_out" else zs)[:, b, h, cols(k)]], func=ACT.Silu if k < NCH else None)
                elif name == "silu_tables":
                    silu_sin_tables()
                elif name == "exp_tables":
                    exp_tables()
                elif name == "silu":
                    act.wait_ge(side_copied, DONE["x1", k + 1])
                    silu_sin_tables()
                    s.activation(u[:, b, :, :], u[:, b, :, :], ACT.Silu).then_inc(u_ready, 1)
                    exp_tables()
                elif name == "xdb_out":
                    if k >= NCH:
                        act.wait_ge(c_stored, 16 * (k - NCH + 1))
                    copy_out(("xdb", k), [xdb[:, cols(k)]], rows=RANK + 2 * NST)
                elif name == "dt_out":
                    h = args[0]
                    if k >= NCH:
                        act.wait_ge(du_ready, k - NCH + 1)
                    copy_out((f"dt{h}", k), [ebuf[:, h, cols(k)]], bias=bdt_sb[:, h:h + 1])
                elif name == "b3_out":
                    copy_out(("b3", k), [b3_full(k)], rows=B3)
                elif name == "b3_high":
                    act.wait_ge(side_copied, DONE["b3", k])
                    s.copy(b3[:, b, cols(k)], b3_full(k)).then_inc(b3_high, 1)
                elif name == "b3_mid":
                    act.wait_ge(b3_rest_ready, k + 1)
                    s.copy(b3[32:64, b, cols(k)], b3_rest[32:64, :]).then_inc(b3_mid_ready, 1)
                    s.copy(b3_mid[64:96, :], b3_rest[64:96, :]).then_inc(b3_mid_ready, 1)
                elif name == "tail":
                    softplus(k, *args)

            def softplus(k, p):
                b, lo, hi = k // NCH, cols(k).start, cols(k).stop
                if p == 0:
                    act.wait_ge(side_copied, DONE["dt1", k])
                    chain.add(s.activation(sbuf_[:, :, lo:hi], ebuf[:, :, lo:hi], ACT.Abs))
                elif p == 1:
                    chain.wait()
                    act.wait_ge(relu_part, k + 1)
                    chain.add(s.activation(ebuf[:, :, lo:hi], sbuf_[:, :, lo:hi], ACT.Exp, scale=-1.0))
                elif p == 2:
                    chain.wait()
                    chain.add(s.activation(sbuf_[:, :, lo:hi], ebuf[:, :, lo:hi], ACT.Ln, bias=two[:, :]))
                elif p == 3:
                    chain.wait()
                    s.activation(sbuf_[:, :, lo:hi], sbuf_[:, :, lo:hi], ACT.Exp, scale=-1.0).then_inc(e_ready, 1)
                elif p == 5:
                    act.wait_ge(s_ready, k + 1)
                    s.activation(s2buf[:, :, lo:hi], sbuf_[:, :, lo:hi], ACT.Square).then_inc(s2_ready, 1)

            def beside(n):
                for st in BESIDE[n]:
                    step(*st)

            def decays(q, i, r):
                b, c = q // NCH, q % NCH
                k = i * (2 * NPT) + (q * STEPS + 2 * r)
                for h in range(EH):
                    if not (q == 0 and is0(i) and r == 0):
                        act.wait_ge(h_ready, k + (h - 1))
                    s.activation(ps[:, DA + h, :], delta[:, b, h, c * CH:(c + 1) * CH], ACT.Exp,
                                 scale=a_sb[:, h, bass.ds(i * NPT + r, 1)]).then_inc(dA_ready, 1)
                    if c == 0 and not (is0(i) and r == 0):
                        sl = (2 * r + h - 2) % SLOTS
                        s.copy(state[:, bass.ds(i * (2 * NPT) + (2 * r + h - 2), 1)], hs[:, sl, CH - 1:CH])

            def last_states(q):
                for j in range(STEPS - 2, STEPS):
                    act.wait_ge(h_ready, q * STEPS + j + 1)
                    chain.add(s.copy(state[:, j:j + 1], hs[:, j % SLOTS, CH - 1:CH]))

            def mamba_out(q):
                copy_out(("out", q), [y2[:, 0, :]])

            def ffn(groups, aside):
                units = [FC * g_ + f for g_ in groups for f in range(FC)]
                if groups[0] == 0:
                    s.activation(zs[:, 1, :, :], zs[:, 1, :, :], ACT.Silu).then_inc(z_ready, 1)

                def evict(U):
                    act.wait_ge(hid_in_psum, U + 1)
                    if U >= SLOTS:
                        act.wait_ge(q_ready, U - SLOTS + 1)
                    s.activation(hid[:, U % SLOTS, :], ps[:, UP + U % 2, :], ACT.Identity,
                                 bias=b1_sb[:, U % FC:U % FC + 1]).then_inc(hid_ready, 1)

                def turns(U):
                    act.wait_ge(arg_ready, U + 1)
                    s.activation(turn[:, U % SLOTS, :], tbuf[:, U % SLOTS, :], ACT.Identity, bias=rho_turns[:, U % FC:U % FC + 1],
                                 scale=INV_2PI).then_inc(turns_ready, 1)

                def sine(U):
                    act.wait_ge(part_ready, U + 1)
                    s.activation(sn[:, U % SLOTS, :], jbuf[:, U % SLOTS, :], ACT.Sin, scale=2 * PI_LO).then_inc(sin_ready, 1)

                def relu(U):
                    act.wait_ge(q_ready, U + 1)
                    s.activation(act_sb[:, U % SLOTS, :], act_sb[:, U % SLOTS, :], ACT.Relu).then_inc(act_ready, 1)

                for n in range(len(units) + 3):
                    aside(n)
                    if n < len(units):
                        evict(units[n])
                    if n >= 1 and n - 1 < len(units):
                        turns(units[n - 1])
                    if n >= 2 and n - 2 < len(units):
                        sine(units[n - 2])
                    if n >= 3:
                        relu(units[n - 3])

            def qkv_copies(b, h):
                copy_out(("qkv", (b, h)), [qT(b)[:, cols(h)], kT(b)[:, cols(h)], flat(vt[:, h * HT:(h + 1) * HT, :])])

            def probabilities(J, par, bank, reuse):
                act.wait_ge(negm_ready, J + 1)
                if reuse:
                    act.wait_ge(pT_in_psum, (J - reuse) * 2 + 2)
                    act.wait_ge(rinv_ready, J - reuse + 1)
                s.activation(pm[:, par, :], flat(ps[:, bank:bank + 2, :]), ACT.Exp, bias=negm[:, par:par + 1],
                             scale=QK, accum_out=rsum[:, par:par + 1]).then_inc(probs_ready, 1)

            def pT_copy(J, par, low, high, reuse):
                act.wait_ge(pT_in_psum, J * 2 + 1)
                if reuse:
                    act.wait_ge(attn_out, J - reuse + 1)
                s.copy(flat(pT[:, par, 0:4, :]), ps[:, low, :]).then_inc(pT_low, 1)
                if high is not None:
                    act.wait_ge(pT_in_psum, J * 2 + 2)
                    s.copy(flat(pT[:, par, 4:8, :]), ps[:, high, :]).then_inc(pT_high, 1)

            exp_tables()
            act.wait_ge(consts_made, 1)
            act.wait_ge(small_w_loaded, 16 * N_SMALL)
            s.activation(a_sb[:, :, :], a_sb[:, :, :], ACT.Exp).then_inc(a_exp, 1)
            silu_sin_tables()
            for st in TURN_FIRST:
                step(*st)
            act.wait_ge(trig_args, 1)
            s.activation(trig[:, 4:6, :], trig[:, 0:2, :], ACT.Sin).then_inc(trig_done, 1)
            for st in ALONE:
                step(*st)
            act.wait_ge(a_ready, 1)
            for q in range(NCH):
                act.wait_ge(du_ready, q + 1)
                for n in range(NST):
                    decays(q, n // NPT, n % NPT)
                    if q and n == 0:
                        last_states(q - 1)
                    beside(NST * q + n)
                    if q and n == 6:
                        mamba_out(q - 1)

            def aside(n):
                if n == 3:
                    mamba_out(1)
                elif n == 4:
                    half_turned(1)
            silu_sin_tables()
            ffn((0, 1), aside)
            exp_tables()
            half_turned(2)
            qkv_copies(0, 0)
            half_turned(3)
            act.wait_ge(out_read, 2)
            for q in range(NCH, 2 * NCH):
                act.wait_ge(du_ready, q + 1)

                def tile(i, first, first_tile, out_copy=False):
                    J = i + (q - NCH) * NPT
                    for r in range(NPT):
                        decays(q, i, r)
                        if r == 2:
                            probabilities(J, 0, SIDE, 0 if first else 1)
                        if out_copy and r == 1:
                            mamba_out(q - 1)
                        if first and r == 0:
                            qkv_copies(0, 1)
                        if q > NCH and first_tile and r == 0:
                            last_states(q - 1)
                        if r == 3:
                            pT_copy(J, 0, SIDE, SIDE + 1, 0 if first else 1)
                tile(0, q == NCH, True)
                tile(1, False, False, q > NCH)
                with act.Fori(2, NST // NPT) as i:
                    tile(i, False, False)
            silu_sin_tables()
            half_turned(4)

            def aside(n):
                if n == 2:
                    half_turned(5)
                elif n == 4:
                    mamba_out(2 * NCH - 1)
                elif n == 7:
                    half_turned(6)
                elif n == 11:
                    half_turned(7)
                elif n == 18:
                    half_turned(8)
            ffn((2, 3, 4, 5), aside)
            exp_tables()
            qkv_copies(1, 0)
            half_turned(9)
            qkv_copies(1, 1)
            for par in range(2):
                probabilities(TILES + par, par, 2 * par, 2)
            with act.Fori(0, TILES // 2 - 1) as i:
                for par in range(2):
                    J = i * 2 + (TILES + par)
                    pT_copy(J, par, 4, None, 2)
                    probabilities(J + 2, par, 2 * par, 2)
            pT_copy(2 * TILES - 2, 0, 4, None, 2)
            silu_sin_tables()
            pT_copy(2 * TILES - 1, 1, 4, None, 2)
            half_turned(10)

            def aside(n):
                if n == 3:
                    half_turned(11)
            ffn((6, 7), aside)

        @block.vector
        def _(dve):
            chain = Chain(dve, dve_chain)
            v_ = nc.vector

            def root_part(k, dst, lo, hi):
                v, y, t = var_eps[:, lo:hi], rstd0[:, lo:hi], newton[:, lo:hi]
                chain.wait()
                if k == 0:
                    ins = v_.tensor_scalar(y.bitcast(I32), v.bitcast(I32), 1, None, ALU.arith_shift_right)
                elif k == 1:
                    ins = v_.tensor_scalar(y.bitcast(I32), y.bitcast(I32), -1, ROOT_GUESS, ALU.mult, ALU.add)
                elif k % 3 == 2:
                    ins = v_.scalar_tensor_tensor(t, y, -0.5, y, ALU.mult, ALU.mult)
                elif k % 3 == 0:
                    ins = v_.tensor_tensor(t, t, v, ALU.mult)
                else:
                    ins = v_.scalar_tensor_tensor(y if k < 10 else dst[:, lo:hi], t, 1.5, y, ALU.add, ALU.mult)
                chain.add(ins)

            def inverse_root(dst, lo, hi):
                for k in range(11):
                    root_part(k, dst, lo, hi)
                chain.wait()

            def moments_part(k, b, lo, hi):
                xb = x_of(b)
                if k < 2:
                    for t in range(lo, hi):
                        if k == 0:
                            chain.add(v_.bn_stats(stats[:, t, :], xb[:, t, :]))
                        else:
                            if t == lo:
                                chain.wait()
                            chain.add(v_.bn_aggr(mv[:, t, :], stats[:, t, :]))
                else:
                    chain.wait()
                    chain.add(v_.tensor_scalar(var_eps[:, lo:hi], mv[:, lo:hi, 1], LN_EPS, None, ALU.add))

            def moments(b, lo, hi):
                for k in range(3):
                    moments_part(k, b, lo, hi)

            def normalise(b, dst, scale, lo, hi, signal, every):
                for t in range(lo, hi):
                    ins = v_.tensor_scalar(dst[:, t, :], x_of(b)[:, t, :], mv[:, t, 0:1], scale[:, t:t + 1],
                                           ALU.subtract, ALU.mult)
                    if t % every == every - 1:
                        ins.then_inc(signal, 1)

            def half_norm(i, parts=range(NORM_PARTS)):
                _, b, h = HALVES[i]
                lo, hi = h * HT, (h + 1) * HT
                for k in parts:
                    if k < 3:
                        moments_part(k, b, lo, hi)
                    elif k < NORM_PARTS - 1:
                        root_part(k - 3, rstd, lo, hi)
                    else:
                        last = max([-1] + [j for j in range(i) if HALVES[j][2] == h])
                        dve.wait_ge(side_filled, DONE["half", last] if last >= 0 else DONE["turn", NCH + h])
                        chain.wait()
                        normalise(b, xn, rstd, lo, hi, xn_ready, HT)

            def norm_step(b, p):
                if p == 0:
                    dve.wait_ge(x_loaded[b], 16)
                    moments(b, 0, TILES)
                elif p == 2:
                    inverse_root(rstd, 0, TILES)
                    chain.link(v_.tensor_tensor(newton[:, :], rstd[:, :], rstd[:, :], ALU.mult))
                    chain.link(v_.tensor_tensor(newton[:, :], newton[:, :], mv[:, :, 1], ALU.mult))
                    chain.link(v_.tensor_scalar(var_eps[:, :], newton[:, :], RMS_EPS, None, ALU.add))
                elif p == 5:
                    dve.wait_ge(*((x_added, 1) if b else (wconv_ready, 1)))
                    normalise(b, x1, rstd, 0, TILES, x1_ready, TILES)
                elif p == 4:
                    inverse_root(rstd2, 0, TILES)
                    chain.link(v_.tensor_tensor(rstd2[:, :], rstd2[:, :], rstd[:, :], ALU.mult))
                    normalise(b, xn, rstd2, 0, TILES, xn_ready, HT)

            def step(name, k, *args):
                b = k // NCH
                if name == "norm":
                    norm_step(k, *args)
                elif name == "half_norm":
                    half_norm(k, args)
                elif name == "b3_rest":
                    dve.wait_ge(b3_high, k + 1)
                    if k:
                        dve.wait_ge(b3_ready, k)
                    v_.tensor_tensor(b3_rest[:, :], b3_full(k), b3[:, b, cols(k)], ALU.subtract).then_inc(b3_rest_ready, 1)
                elif name == "b3_low":
                    dve.wait_ge(b3_mid_ready, 2 * k + 2)
                    v_.tensor_tensor(b3[64:96, b, cols(k)], b3_rest[64:96, :], b3_mid[64:96, :], ALU.subtract).then_inc(b3_ready, 1)
                elif name == "tail":
                    softplus(k, *args)

            def softplus(k, p):
                b, lo, hi = k // NCH, cols(k).start, cols(k).stop

                def cut(t):
                    return t[:, :, lo:hi]
                e, v1, v2 = cut(ebuf), cut(sbuf_), cut(s2buf)
                dl = delta[:, b, :, lo:hi]
                if p == 0:
                    dve.wait_ge(side_copied, DONE["dt1", k])
                    v_.tensor_scalar(dl, e, 0.0, None, ALU.max).then_inc(relu_part, 1)
                elif p == 4:
                    dve.wait_ge(e_ready, k + 1)
                    v_.tensor_tensor(v1, e, v1, ALU.mult).then_inc(s_ready, 1)
                elif p == 6:
                    dve.wait_ge(s2_ready, k + 1)
                    chain.add(v_.tensor_scalar(e, v2, ATANH[4], ATANH[3], ALU.mult, ALU.add))
                elif p == 7:
                    chain.wait()
                    chain.add(v_.tensor_tensor(e, e, v2, ALU.mult))
                elif p in (8, 9, 10):
                    chain.wait()
                    for h in range(EH):
                        chain.add(v_.scalar_tensor_tensor(e[:, h, :], e[:, h, :], ATANH[10 - p], (v1 if p == 10 else v2)[:, h, :], ALU.add, ALU.mult))
                elif p == 11:
                    chain.wait()
                    ins = v_.tensor_tensor(dl, dl, e, ALU.add)
                    if k >= NCH:
                        ins.then_inc(delta_ready, 1)
                    else:
                        chain.add(ins)
                elif p == 12 and k < NCH:
                    chain.wait()
                    v_.tensor_tensor(du[:, b, :, lo:hi], dl, u[:, b, :, lo:hi], ALU.mult).then_inc(du_ready, 1)

            def beside(n):
                for st in BESIDE[n]:
                    step(*st)

            def drive(q, i, r):
                b, c = q // NCH, q % NCH
                for h in range(EH):
                    if h == 0:
                        dve.wait_ge(B_ready, i * NPT + (q * NST + r + 1))
                    if not (q == 0 and is0(i) and r < 2):
                        dve.wait_ge(h_ready, i * (2 * NPT) + (q * STEPS + 2 * r + h + 1 - SLOTS))
                    v_.tensor_tensor(dbu[:, (2 * r + h) % SLOTS, :], ps[:, BB, :], du[:, b, h, c * CH:(c + 1) * CH], ALU.mult)\
                        .then_inc(dbu_ready, 1)

            def scan(q, i, r):
                c = q % NCH
                k = i * (2 * NPT) + (q * STEPS + 2 * r)
                for h in range(EH):
                    sl = (2 * r + h) % SLOTS
                    dve.wait_ge(dbu_ready, k + (h + 1))
                    dve.wait_ge(dA_ready, k + (h + 1))
                    if not (q == 0 and is0(i) and r < 2):
                        dve.wait_ge(prod_ready, k + (h + 1 - SLOTS))
                    initial = 0.0 if c == 0 else state[:, bass.ds(i * (2 * NPT) + (2 * r + h), 1)]
                    v_.tensor_tensor_scan(hs[:, sl, :], ps[:, DA + h, :], dbu[:, sl, :], initial, ALU.mult, ALU.add)\
                        .then_inc(h_ready, 1)

            def first_drive(q):
                dve.wait_ge(du_ready, q + 1)
                drive(q, 0, 0)

            def scan_state(q, i, r):
                if not (isinstance(i, int) and i * NPT + r == NST - 1):
                    drive(q, i + (r + 1) // NPT, (r + 1) % NPT)
                scan(q, i, r)

            def gate(q):
                b, c = q // NCH, q % NCH
                dve.wait_ge(y_added, STEPS * (q + 1))
                if q >= NCH:
                    dve.wait_ge(z_ready, 1)
                for h in range(EH):
                    v_.tensor_tensor(y2[:, h, :], ps[:, YY + h, :], zs[:, b, h, c * CH:(c + 1) * CH], ALU.mult).then_inc(y2_ready, 1)

            def add_mamba(q):
                b, c = q // NCH, q % NCH
                dve.wait_ge(side_copied, DONE["out", q])
                dve.wait_ge(x_added, b + 1)
                xs = flat(x_of(b)[:, TPC * c:TPC * (c + 1), :])
                chain.link(v_.tensor_tensor(xs, y2[:, 0, :], xs, ALU.add))

            def ffn(groups, aside):
                units = [FC * g_ + f for g_ in groups for f in range(FC)]

                def arg(U):
                    sl, f = U % SLOTS, U % FC
                    dve.wait_ge(hid_ready, U + 1)
                    v_.tensor_scalar(tbuf[:, sl, :], hid[:, sl, :], 0.1, theta[:, f:f + 1], ALU.mult, ALU.add).then_inc(sum_ready, 1)

                def arg_less_theta(U):
                    sl, f = U % SLOTS, U % FC
                    dve.wait_ge(sum_ready, U + 1)
                    v_.tensor_scalar(tbuf[:, sl, :], tbuf[:, sl, :], theta[:, f:f + 1], None, ALU.subtract).then_inc(arg_ready, 1)

                def whole_turns(U):
                    sl = U % SLOTS
                    dve.wait_ge(turns_ready, U + 1)
                    v_.tensor_scalar(jbuf[:, sl, :], turn[:, sl, :], ROUND, ROUND, ALU.add, ALU.subtract).then_inc(whole_ready, 1)

                def quantum(U):
                    sl, f = U % SLOTS, U % FC
                    dve.wait_ge(sin_ready, U + 1)
                    if U >= SLOTS:
                        dve.wait_ge(act_used, U - SLOTS + 1)
                    v_.scalar_tensor_tensor(act_sb[:, sl, :], sn[:, sl, :], coef[:, f:f + 1], hid[:, sl, :], ALU.mult, ALU.add)\
                        .then_inc(q_ready, 1)

                def add_out(g_):
                    norm, b, h = GROUPS[g_]
                    dve.wait_ge(act_used, FC * (g_ + 1))
                    dve.wait_ge(x_added, BATCH + g_ + 1)
                    xs = flat(half_of(b, h))
                    v_.tensor_tensor(xs, ps[:, SUM[g_ % 2], :], xs, ALU.add).then_inc(out_read, 1)
                    dve.wait_ge(out_read, g_ + 1)
                    if norm == "norm4":
                        v_.engine_nop().then_inc(x_final, 1)

                n_units = len(units)
                for n in range(n_units + 5):
                    aside(n, 0)
                    if n < n_units:
                        arg(units[n])
                    aside(n, 1)
                    if n >= 1 and n - 1 < n_units:
                        whole_turns(units[n - 1])
                    aside(n, 2)
                    if n >= 2 and n - 2 < n_units:
                        quantum(units[n - 2])
                    aside(n, 3)
                    if n < n_units:
                        arg_less_theta(units[n])
                    if n >= 5 and units[n - 5] % FC == FC - 1:
                        add_out(units[n - 5] // FC)

            def row_max(J, par, bank):
                dve.wait_ge(scores_ready, J + 1)
                v_.tensor_reduce(mx[:, par:par + 1], flat(ps[:, bank:bank + 2, :]), AX_X, ALU.max).then_inc(mx_ready, 1)
                dve.wait_ge(mx_ready, J + 1)
                v_.tensor_scalar(negm[:, par:par + 1], mx[:, par:par + 1], -QK, None, ALU.mult).then_inc(negm_ready, 1)

            def invert_sum(J, par, reuse):
                dve.wait_ge(probs_ready, J + 1)
                if reuse:
                    dve.wait_ge(attn_added, J - reuse + 1)
                v_.reciprocal(rinv[:, par:par + 1], rsum[:, par:par + 1]).then_inc(rinv_ready, 1)

            def add_attention(J, par, bank):
                dve.wait_ge(rinv_ready, J + 1)
                dve.wait_ge(attn_out, J + 1)
                xs = flat(x_tok[:, bass.ds(J, 1), :])
                v_.scalar_tensor_tensor(xs, ps[:, bank, 0:D], rinv[:, par:par + 1], xs, ALU.mult, ALU.add).then_inc(attn_added, 1)

            v_.memset(xnT[:, :, 0:KCONV - 1], 0.0)
            dve.wait_ge(mamba_w_loaded, 16 * N_MAMBA)
            v_.tensor_scalar(win_sb[:, :], win_sb[:, :], normw_sb[:, :], None, ALU.mult).then_inc(win_scaled, 1)
            step(*NORM_FIRST[0])
            dve.wait_ge(small_w_loaded, 16 * N_SMALL)
            dve.wait_ge(win_scaled, 1)
            for tap in range(KCONV):
                ins = v_.tensor_tensor(wconv[:, tap, :], win_sb[:, 0:E], convw_sb[:, tap::KCONV], ALU.mult)
            ins.then_inc(wconv_ready, 1)
            for st in NORM_FIRST[1:] + TURN_FIRST:
                step(*st)
            kk, r = trig[:, 2, :], trig[:, 3, :]
            chain.link(v_.tensor_scalar(kk, theta[:, :], INV_2PI, ROUND, ALU.mult, ALU.add))
            chain.link(v_.tensor_scalar(kk, kk, ROUND, None, ALU.subtract))
            chain.link(v_.scalar_tensor_tensor(r, kk, -C1, theta[:, :], ALU.mult, ALU.add))
            chain.link(v_.scalar_tensor_tensor(r, kk, -C2, r, ALU.mult, ALU.add))
            chain.link(v_.scalar_tensor_tensor(rho[:, :], kk, -C3, r, ALU.mult, ALU.add))
            chain.link(v_.tensor_scalar(kk, rho[:, :], np.pi / 2, None, ALU.add))
            chain.link(v_.tensor_scalar(r, kk, np.pi, -TWO_PI, ALU.is_gt, ALU.mult))
            chain.link(v_.tensor_tensor(kk, kk, r, ALU.add))
            chain.add(v_.tensor_scalar(rho_turns[:, :], rho[:, :], INV_2PI, None, ALU.mult))
            chain.add(v_.tensor_scalar(trig[:, 0, :], rho[:, :], PI_LO, -PI_LO, ALU.min, ALU.max))
            v_.tensor_scalar(trig[:, 1, :], kk, PI_LO, -PI_LO, ALU.min, ALU.max).then_inc(trig_args, 1)
            dve.wait_ge(a_exp, 1)
            v_.tensor_scalar(a_sb[:, :, :], a_sb[:, :, :], -1.0, None, ALU.mult).then_inc(a_ready, 1)
            dve.wait_ge(consts_made, 2)
            for h in range(EH):
                v_.tensor_scalar(diag_d[:, h, :], ident[:, :], dpar_sb[:, h:h + 1], None, ALU.mult).then_inc(diag_ready, 1)
            dve.wait_ge(late_w_loaded, 16 * N_LATE)
            dve.wait_ge(trig_done, 1)
            chain.link(v_.tensor_tensor(trig[:, 6, :], trig[:, 5, :], wr_sb[:, :], ALU.mult))
            chain.link(v_.tensor_tensor(trig[:, 7, :], trig[:, 4, :], wi_sb[:, :], ALU.mult))
            chain.link(v_.tensor_tensor(trig[:, 6, :], trig[:, 6, :], trig[:, 7, :], ALU.add))
            chain.link(v_.tensor_tensor(trig[:, 6, :], trig[:, 6, :], wi_sb[:, :], ALU.mult))
            chain.link(v_.tensor_scalar(coef[:, :], trig[:, 6, :], 0.1, None, ALU.mult))
            for st in ALONE:
                step(*st)
            first_drive(0)
            for q in range(NCH):
                for n in range(NST):
                    scan_state(q, n // NPT, n % NPT)
                    beside(NST * q + n)
                    if q and n == 1:
                        gate(q - 1)
                    if q and n == 8:
                        add_mamba(q - 1)
                if q < NCH - 1:
                    first_drive(q + 1)

            def aside(n, j):
                if j:
                    return
                if n == 1:
                    gate(NCH - 1)
                elif n == 3:
                    add_mamba(NCH - 1)
                    half_norm(1)
                elif n == 10:
                    half_norm(2)
            ffn((0, 1), aside)
            half_norm(3)
            first_drive(NCH)
            for q in range(NCH, 2 * NCH):
                def tile(i, first, first_tile, last):
                    J = i + (q - NCH) * NPT
                    for r in range(NPT):
                        scan_state(q, NST // NPT - 1 if last else i, r)
                        if last and q > NCH:
                            if r == 2:
                                add_mamba(q - 1)
                            parts = range(8 * (r % 2), min(8 * (r % 2) + 8, NORM_PARTS - r // 2))
                            half_norm(4 + r // 2, parts)
                        if q > NCH and first_tile and r == 1:
                            gate(q - 1)
                        if r == 1:
                            row_max(J, 0, SIDE)
                        if r == 2 and not first:
                            add_attention(J - 1, 0, SIDE + 2)
                        if r == 3:
                            invert_sum(J, 0, 0 if first else 1)
                tile(0, q == NCH, True, False)
                with dve.Fori(1, NST // NPT - 1) as i:
                    tile(i, False, False, False)
                tile(NST // NPT - 1, False, False, True)
                if q < 2 * NCH - 1:
                    first_drive(q + 1)

            def norm_aside(i, turn0, n, j, rate=1):
                k = (n - turn0) * 4 + j
                if k >= 0:
                    half_norm(i, range(min(rate * k, NORM_PARTS), min(rate * (k + 1), NORM_PARTS)))

            def aside(n, j):
                if (n, j) == (0, 0):
                    half_norm(5, [NORM_PARTS - 1])
                    add_attention(TILES - 1, 0, SIDE + 2)
                    dve.wait_ge(attn_added, TILES)
                elif (n, j) == (1, 0):
                    gate(2 * NCH - 1)
                elif (n, j) == (4, 3):
                    add_mamba(2 * NCH - 1)
                for i, turn0 in ((6, 1), (7, 5), (8, 13)):
                    norm_aside(i, turn0, n, j)
            ffn((2, 3, 4, 5), aside)
            half_norm(9)

            def turned(J, par):
                dve.wait_ge(pT_in_psum, J * 2 + 2)
                dve.wait_ge(attn_out, J - 1)
                v_.tensor_copy(flat(pT[:, par, 4:8, :]), ps[:, 5, :]).then_inc(pT_high, 1)
                invert_sum(J, par, 2)

            for par in range(2):
                row_max(TILES + par, par, 2 * par)
            with dve.Fori(0, TILES // 2 - 1) as i:
                for par in range(2):
                    J = i * 2 + (TILES + par)
                    turned(J, par)
                    row_max(J + 2, par, 2 * par)
                    add_attention(J, par, 6 + par)
            dve.wait_ge(attn_added, TILES + HT)
            half_norm(10, range(0, 2))
            turned(2 * TILES - 2, 0)
            half_norm(10, range(2, NORM_PARTS - 1))
            add_attention(2 * TILES - 2, 0, 6)
            half_norm(10, [NORM_PARTS - 1])
            turned(2 * TILES - 1, 1)
            add_attention(2 * TILES - 1, 1, 7)

            dve.wait_ge(attn_added, 2 * TILES)

            def aside(n, j):
                norm_aside(11, 0, n, j, 2)
            ffn((6, 7), aside)

        @block.tensor
        def _(pe):
            mm = nc.tensor.matmul

            def side_bank(use, t):
                w = FIRST[use] + t
                if BEFORE[w]:
                    pe.wait_ge(side_copied, BEFORE[w])
                return BANK[w]

            def half_turn(i):
                h = HALVES[i][2]
                pe.wait_ge(xn_ready, 2 * BATCH + i + 1)
                bank = side_bank(("half", i), 0)
                for t in range(HT):
                    ins = nc.tensor.transpose(ps[:, bank, t * P:(t + 1) * P], xn[:, h * HT + t, :], ident[:, :])
                ins.then_inc(side_filled, 1)

            def step(name, k, *args):
                b, c = k // NCH, k % NCH
                if name == "turn":
                    pe.wait_ge(xn_ready, NCH * b + c + 1)
                    bank = side_bank((name, k), 0)
                    for i in range(TPC):
                        ins = nc.tensor.transpose(ps[:, bank, i * P:(i + 1) * P], xn[:, TPC * c + i, :], ident[:, :])
                    ins.then_inc(side_filled, 1)
                elif name == "half_turn":
                    half_turn(k)
                elif name == "x":
                    h, part = args
                    use = (f"x{h}", k)
                    if h == 0 and part == 0:
                        pe.wait_ge(side_copied, DONE["turn", k])
                    bank = BANK[FIRST[use]] if part else side_bank(use, 0)
                    for tap in (2 * part, 2 * part + 1):
                        ins = mm(ps[:, bank, :], wconv_v[:, tap, h, :], xnT[:, b, tap + c * CH:tap + (c + 1) * CH],
                                 start=(tap == 0), stop=(tap == KCONV - 1))
                    if part:
                        ins.then_inc(side_filled, 1)
                elif name == "z":
                    h = args[0]
                    mm(ps[:, side_bank((f"z{h}", k), 0), :], win_v[:, 1, h, :], xT_of(b)[:, cols(k)], start=True, stop=True)\
                        .then_inc(side_filled, 1)
                elif name in ("xdb", "b3"):
                    if name == "xdb":
                        pe.wait_ge(*((u_ready, 1) if k >= NCH else (side_copied, DONE["x1", k])))
                    elif k == 0:
                        pe.wait_ge(wb3_ready, 1)
                    w, rows = (wx_sb, RANK + 2 * NST) if name == "xdb" else (wb3_sb, B3)
                    bank = side_bank((name, k), 0)
                    for h in range(EH):
                        ins = mm(ps[0:rows, bank, :], w[:, h, :], u[:, b, h, cols(k)], start=(h == 0), stop=(h == EH - 1))
                    ins.then_inc(side_filled, 1)
                elif name == "dt":
                    h = args[0]
                    if h == 0:
                        pe.wait_ge(side_copied, DONE["xdb", k])
                    mm(ps[:, side_bank((f"dt{h}", k), 0), :], wdt_v[:, h, :], xdb[0:RANK, cols(k)], start=True, stop=True)\
                        .then_inc(side_filled, 1)

            def beside(n):
                for st in BESIDE[n]:
                    step(*st)

            def b_row(q, i, r):
                b, c = q // NCH, q % NCH
                if not (q == 0 and is0(i) and r == 0):
                    pe.wait_ge(dbu_ready, i * (2 * NPT) + (q * STEPS + 2 * r))
                mm(ps[:, BB, :], flat(bsel[:, bass.ds(i * NPT + r, 1), :]), b3[:, b, c * CH:(c + 1) * CH],
                   start=True, stop=True).then_inc(B_ready, 1)

            def y_sum(q, i, r):
                for h in range(EH):
                    pe.wait_ge(prod_ready, i * (2 * NPT) + (q * STEPS + 2 * r + h + 1))
                    mm(ps[:, YY + h, :], ident[:, :], prod[:, (2 * r + h) % SLOTS, :], start=is0(i) and r == 0, stop=True,
                       skip_group_check=True).then_inc(y_added, 1)

            def y_of_u(q, h):
                b, c = q // NCH, q % NCH
                mm(ps[:, YY + h, :], diag_d[:, h, :], u[:, b, h, c * CH:(c + 1) * CH], start=False, stop=True, skip_group_check=True)

            def scan_state(q, i, r):
                state_n = i * NPT + r if isinstance(i, int) else None
                if state_n == 0 and q % NCH == 0:
                    pe.wait_ge(b3_ready, q + 1)
                    b_row(q, 0, 0)
                    b_row(q, 0, 1)
                if state_n == 0 and q % NCH:
                    b_row(q, 0, 1)
                if state_n != NST - 2 and state_n != NST - 1:
                    b_row(q, i + (r + 2) // NPT, (r + 2) % NPT)
                if state_n == NST - 1 and q % NCH < NCH - 1:
                    pe.wait_ge(b3_ready, q + 2)
                    b_row(q + 1, 0, 0)
                if state_n == 1 and q:
                    pe.wait_ge(y2_ready, EH * q)
                if state_n in (2, 3):
                    y_of_u(q, state_n - 2)
                if state_n != 0:
                    y_sum(q, i - (1 if r == 0 else 0), (r - 1) % NPT)
                elif q % NCH:
                    y_sum(q - 1, NST // NPT - 1, NPT - 1)

            def project_y(q):
                pe.wait_ge(y2_ready, EH * (q + 1))
                if q >= NCH:
                    pe.wait_ge(attn_added, (q - NCH + 1) * NPT)
                bank = side_bank(("out", q), 0)
                for i in range(TPC):
                    for h in range(EH):
                        ins = mm(ps[:, bank, i * D:(i + 1) * D], y2[:, h, i * P:(i + 1) * P], wout_sb[:, h, :],
                                 start=(h == 0), stop=(h == EH - 1), skip_group_check=True)
                ins.then_inc(side_filled, 1)

            def ffn(groups, aside):
                units = [FC * g_ + f for g_ in groups for f in range(FC)]

                def up(U):
                    _, b, h = GROUPS[U // FC]
                    if U >= 2:
                        pe.wait_ge(hid_ready, U - 1)
                    if U % FC == 0:
                        pe.wait_ge(side_copied, DONE["half", HALVES.index(GROUPS[U // FC])])
                    mm(ps[:, UP + U % 2, :], w1_v[:, U % FC, :], xT_of(b)[:, cols(h)], start=True, stop=True).then_inc(hid_in_psum, 1)

                def down(U):
                    g_, f = U // FC, U % FC
                    pe.wait_ge(act_ready, U + 1)
                    if f == 0 and g_ >= 2:
                        pe.wait_ge(out_read, g_ - 1)
                    for i in range(TPC):
                        ins = mm(ps[:, SUM[g_ % 2], i * D:(i + 1) * D], act_sb[:, U % SLOTS, i * P:(i + 1) * P], w2_sb[:, f, :],
                                 start=(f == 0 and i == 0), stop=(f == FC - 1), skip_group_check=True)
                    ins.then_inc(act_used, 1)

                up(units[0])
                up(units[1])
                for n in range(len(units) + 4):
                    if n >= 4:
                        down(units[n - 4])
                    aside(n)
                    if n + 2 < len(units):
                        up(units[n + 2])

            def qkv(b, h, q=True, kv=True):
                pe.wait_ge(side_copied, DONE["half", HALVES.index(("norm3", b, h))])
                use = ("qkv", (b, h))
                for j, w in enumerate((wq_sb, wk_sb)):
                    if kv if j else q:
                        mm(ps[:, side_bank(use, j), :], w[:, :], xT_of(b)[:, cols(h)], start=True, stop=True).then_inc(side_filled, 1)
                if not kv:
                    return
                bank = side_bank(use, 2)
                for t in range(HT):
                    ins = mm(ps[:, bank, t * D:(t + 1) * D], xT_of(b)[:, (h * HT + t) * P:(h * HT + t + 1) * P], wv_sb[:, :],
                             start=True, stop=True, skip_group_check=True)
                ins.then_inc(side_filled, 1)

            def scores(kt, b, bank, halves=(0, 1)):
                for t in halves:
                    ins = mm(ps[:, bank + t, :], kt, qT(b)[:, t * CH:(t + 1) * CH], start=True, stop=True)
                if 1 in halves:
                    ins.then_inc(scores_ready, 1)

            def turn_probs(J, par, banks, reuse):
                pe.wait_ge(probs_ready, J + 1)
                for t in range(2):
                    if reuse:
                        pe.wait_ge(pT_low if t == 0 else pT_high, J)
                    for i in range(4):
                        ins = nc.tensor.transpose(ps[:, banks + t, i * P:(i + 1) * P], pm[:, par, (4 * t + i) * P:(4 * t + i + 1) * P], ident[:, :])
                    ins.then_inc(pT_in_psum, 1)

            def p_v(J, par, bank, reuse):
                pe.wait_ge(pT_low, J + 1)
                pe.wait_ge(pT_high, J + 1)
                if reuse == 1:
                    pe.wait_ge(rinv_ready, J + 1)
                elif reuse:
                    pe.wait_ge(attn_added, J - reuse + 1)
                for i in range(TILES):
                    ins = mm(ps[:, bank, 0:D], pT[:, par, i, :], vt[:, i, :], start=(i == 0), stop=(i == TILES - 1))
                ins.then_inc(attn_out, 1)

            pe.wait_ge(consts_made, 2)
            pe.wait_ge(mamba_w_loaded, 16 * N_MAMBA)
            pe.wait_ge(win_scaled, 1)
            pe.wait_ge(wconv_ready, 1)
            for st in TURN_FIRST + ALONE:
                step(*st)
            pe.wait_ge(consts_made, 3)
            pe.wait_ge(diag_ready, EH)
            for q in range(NCH):
                for n in range(NST):
                    scan_state(q, n // NPT, n % NPT)
                    beside(NST * q + n)
                    if q and n == 5:
                        project_y(q - 1)
            pe.wait_ge(late_w_loaded, 16 * N_LATE)
            pe.wait_ge(h_ready, STEPS * NCH)

            def aside(n):
                if n == 0:
                    y_sum(NCH - 1, NST // NPT - 1, NPT - 1)
                elif n == 1:
                    project_y(NCH - 1)
                elif n == 2:
                    half_turn(1)
            ffn((0, 1), aside)
            half_turn(2)
            qkv(0, 0)
            half_turn(3)
            pe.wait_ge(hid_ready, 2 * FC)
            pe.wait_ge(out_read, 2)
            for q in range(NCH, 2 * NCH):
                def tile(i, first, first_tile):
                    J = i + (q - NCH) * NPT
                    for r in range(NPT):
                        scan_state(q, i, r)
                        if r == 1 and not first:
                            if q > NCH:
                                pe.wait_ge(side_copied, DONE["out", NCH] if not first_tile else DONE["qkv", (0, 1)])
                            p_v(J - 1, 0, SIDE + 2, 1)
                        if first and r == 0:
                            qkv(0, 1)
                            pe.wait_ge(side_copied, DONE["qkv", (0, 1)])
                        if r == 0:
                            pe.wait_ge(kstat_ready, J + 1)
                            if not first:
                                pe.wait_ge(pT_high, J)
                            scores(kstat[:, :], 0, SIDE)
                        if r == 2:
                            turn_probs(J, 0, SIDE, 0)
                        if r == 3 and q > NCH and first_tile:
                            project_y(q - 1)
                tile(0, q == NCH, True)
                with pe.Fori(1, NST // NPT - 1) as i:
                    tile(i, False, False)
                tile(NST // NPT - 1, False, False)
            p_v(TILES - 1, 0, SIDE + 2, 1)
            half_turn(4)
            pe.wait_ge(h_ready, STEPS * NCH * BATCH)

            def aside(n):
                if n == 0:
                    y_sum(2 * NCH - 1, NST // NPT - 1, NPT - 1)
                    half_turn(5)
                elif n == 2:
                    project_y(2 * NCH - 1)
                elif n == 5:
                    half_turn(6)
                elif n == 9:
                    half_turn(7)
                elif n == 17:
                    half_turn(8)
            ffn((2, 3, 4, 5), aside)
            qkv(1, 0)

            def scores1(j, halves=(0, 1)):
                if j >= 2:
                    pe.wait_ge(probs_ready, TILES + j - 1)
                scores(kT(1)[:, j * P:(j + 1) * P], 1, 2 * (j % 2), halves)

            pe.wait_ge(hid_ready, 6 * FC)
            pe.wait_ge(out_read, 6)
            pe.wait_ge(side_copied, FIRST["qkv", (1, 0)] + 2)
            for j in range(2):
                scores1(j, (0,))
            half_turn(9)
            qkv(1, 1, kv=False)
            pe.wait_ge(side_copied, FIRST["qkv", (1, 1)] + 1)
            for j in range(2):
                scores1(j, (1,))
            qkv(1, 1, q=False)
            pe.wait_ge(side_copied, DONE["qkv", (1, 1)])
            for j in range(TILES):
                turn_probs(TILES + j, j % 2, 4, True)
                if j + 2 < TILES:
                    scores1(j + 2)
                if j == TILES - 1:
                    pe.wait_ge(attn_added, TILES + j)
                    half_turn(10)
                p_v(TILES + j, j % 2, 6 + j % 2, 2)

            def aside(n):
                if n == 2:
                    half_turn(11)
            ffn((6, 7), aside)


_INS = ['L0_attn_a_hidden_states', 'L0_attn_a_norm_w', 'L0_attn_a_W_in', 'L0_attn_a_conv_w', 'L0_attn_a_W_x',
        'L0_attn_a_W_dt', 'L0_attn_a_b_dt', 'L0_attn_a_A_log', 'L0_attn_a_D_param', 'L0_attn_a_W_out',
        'L0_attn_b_W_query', 'L0_attn_b_W_key', 'L0_attn_b_W_value', 'L0_ffn_W1', 'L0_ffn_b1',
        'L0_ffn_quantum_phases', 'L0_ffn_quantum_weights_real', 'L0_ffn_quantum_weights_imag', 'L0_ffn_W2', 'L0_ffn_b2']
_OUTS = [((BATCH, SEQ, D), 'float32')]


def kernel(**inputs):
    import concourse.bacc as _bacc
    from concourse.bass_utils import run_bass_kernel_spmd as _run

    nc = _bacc.Bacc("TRN2", target_bir_lowering=False, num_devices=1)
    arrays, args = {}, []
    for name in _INS:
        a = np.ascontiguousarray(inputs[name])
        arrays[f"in_{name}_dram"] = a
        args.append(nc.dram_tensor(f"in_{name}_dram", a.shape, mybir.dt.from_np(a.dtype), kind="ExternalInput").ap())
    for i, (shape, dtype) in enumerate(_OUTS):
        args.append(nc.dram_tensor(f"out_{i}_dram", shape, mybir.dt.from_np(np.dtype(dtype)), kind="ExternalOutput").ap())
    build(nc, *args)
    r = _run(nc, [arrays], core_ids=[0])
    return tuple(r.results[0][f"out_{i}_dram"] for i in range(len(_OUTS)))[0]
```
